# Optimizing a Trainium2 kernel written in Bass

```python
import numpy as np
import jax
import jax.numpy as jnp

def _softmax(x, axis=-1):
    return jax.nn.softmax(x, axis=axis)

def _gelu(x):
    return jax.nn.gelu(x, approximate=True)

def _silu(x):
    return jax.nn.silu(x)

def _sigmoid(x):
    return jax.nn.sigmoid(x)

def _layernorm(x, axis=-1, eps=1e-05):
    m = jnp.mean(x, axis=axis, keepdims=True)
    v = jnp.var(x, axis=axis, keepdims=True)
    return (x - m) / jnp.sqrt(v + eps)

def _scatter_add(tgt, idx, src, axis=0):
    return tgt.at[idx].add(src)

def _segment_sum(src, seg, n):
    return jax.ops.segment_sum(src, seg, n)
kernel_name = 'mk_flamingo_gated_d1_seqx_r4_4e9aef'

def setup_inputs(seed: int=0):
    np.random.seed(seed)
    _w = jnp.asarray

    def _rec_inputs():
        import jax
        import jax.numpy as jnp
        _rk = jax.random.key(seed)
        x = 7.22e-05 + 1 * jax.random.normal(jax.random.fold_in(_rk, 1), (8, 256, 256), jnp.float32)
        _lenS = 256 - jax.random.randint(jax.random.fold_in(_rk, 7), (8,), 0, max(1, 256 // 4) + 1, jnp.int32)
        _lenS2 = 256 - jax.random.randint(jax.random.fold_in(_rk, 8), (8,), 0, max(1, 256 // 4) + 1, jnp.int32)
        _ctx_1024P = jax.random.normal(jax.random.fold_in(_rk, 11), (8, 16, 256), jnp.float32)
        _ctx_1024c = jax.random.dirichlet(jax.random.fold_in(_rk, 511), 0.3 * jnp.ones((16,), jnp.float32), (8, 256))
        _ctx_1024t = jnp.einsum('bsk,bkd->bsd', _ctx_1024c, _ctx_1024P)
        _ctx_1024t = _ctx_1024t * jax.lax.rsqrt(jnp.mean(jnp.square(_ctx_1024t)) + 1e-12) * 0.953939
        ctx_1024 = 4.13588e-05 + 0.999923 * (_ctx_1024t + 0.3 * jax.random.normal(jax.random.fold_in(_rk, 611), (8, 256, 256), jnp.float32))
        _g = jax.random.normal(jax.random.fold_in(_rk, 9001), (2, 1), jnp.float32)
        _g = jnp.sign(_g) * jnp.maximum(jnp.abs(_g), 1.0) + (_g == 0) * 1.0
        g_xattn = _g[0]
        g_ffn = _g[1]
        return (x, ctx_1024, g_xattn, g_ffn)
    x, ctx_1024, g_xattn, g_ffn = _rec_inputs()

    def _L0_xattn_setup():
        import jax, jax.numpy as jnp
        import numpy as np
        HEADS = 16
        D_MODEL = 256
        D_K = D_MODEL // HEADS
        key = jax.random.key(seed)
        ks = jax.random.split(key, 11)
        B, S = (4, 512)
        scale = 1.0 / np.sqrt(D_MODEL)
        inp = {'query': jax.random.normal(ks[0], (B, S, D_MODEL), dtype=jnp.float32), 'key': jax.random.normal(ks[1], (B, S, D_MODEL), dtype=jnp.float32), 'value': jax.random.normal(ks[2], (B, S, D_MODEL), dtype=jnp.float32), 'Wq': jax.random.normal(ks[3], (D_MODEL, D_MODEL), dtype=jnp.float32) * scale, 'bq': jnp.zeros((D_MODEL,), dtype=jnp.float32), 'Wk': jax.random.normal(ks[4], (D_MODEL, D_MODEL), dtype=jnp.float32) * scale, 'bk': jnp.zeros((D_MODEL,), dtype=jnp.float32), 'Wv': jax.random.normal(ks[5], (D_MODEL, D_MODEL), dtype=jnp.float32) * scale, 'bv': jnp.zeros((D_MODEL,), dtype=jnp.float32), 'Wo': jax.random.normal(ks[6], (D_MODEL, D_MODEL), dtype=jnp.float32) * scale, 'bo': jnp.zeros((D_MODEL,), dtype=jnp.float32)}
        return inp
    _L0_xattn_all = _L0_xattn_setup()
    _L0_xattn_in = {k: v for k, v in _L0_xattn_all.items() if k in ('Wq', 'bq', 'Wk', 'bk', 'Wv', 'bv', 'Wo', 'bo')}
    del _L0_xattn_all

    def _L0_ffn_setup():
        import jax, jax.numpy as jnp
        import numpy as np
        B, S, DIM = (4, 1024, 256)
        BASE_COUPLING = 0.1
        NUM_CYCLES = 3

        def _gelu(x):
            return jax.nn.gelu(x, approximate=False)

        def _coupling_net(h, w1, b1, w2, b2, w3, b3, w4, b4):
            h = _gelu(h @ w1 + b1)
            h = _gelu(h @ w2 + b2)
            h = _gelu(h @ w3 + b3)
            return jax.nn.sigmoid(h @ w4 + b4)

        def _global_net(h, w1, b1, w2, b2, w3, b3):
            h = _gelu(h @ w1 + b1)
            h = _gelu(h @ w2 + b2)
            return jax.nn.sigmoid(h @ w3 + b3)

        def _twist(x):
            o_r, o_i, p_r, p_i = jnp.split(x, 4, axis=-1)
            return jnp.concatenate([p_r, -p_i, -o_r, o_i], axis=-1)
        key = jax.random.key(seed)
        ks = jax.random.split(key, 9)
        d = DIM

        def w(k, fan_in, fan_out):
            return jax.random.normal(k, (fan_in, fan_out), dtype=jnp.float32) / np.sqrt(fan_in).astype(np.float32)
        inp = {'x': jax.random.normal(ks[0], (B, S, d), dtype=jnp.float32)}
        cn_dims = [(d, d), (d, d // 2), (d // 2, d // 4), (d // 4, 1)]
        for i, (a, b) in enumerate(cn_dims):
            inp[f'cn_w{i + 1}'] = w(ks[1 + i], a, b)
            inp[f'cn_b{i + 1}'] = jnp.zeros((b,), dtype=jnp.float32)
        gc_dims = [(d, d // 2), (d // 2, d // 4), (d // 4, 1)]
        for i, (a, b) in enumerate(gc_dims):
            inp[f'gc_w{i + 1}'] = w(ks[5 + i], a, b)
            inp[f'gc_b{i + 1}'] = jnp.zeros((b,), dtype=jnp.float32)
        inp['adaptive_range'] = jnp.full((1,), 0.2, dtype=jnp.float32)
        return inp
    _L0_ffn_all = _L0_ffn_setup()
    _L0_ffn_in = {k: v for k, v in _L0_ffn_all.items() if k in ('cn_w1', 'cn_b1', 'cn_w2', 'cn_b2', 'cn_w3', 'cn_b3', 'cn_w4', 'cn_b4', 'gc_w1', 'gc_b1', 'gc_w2', 'gc_b2', 'gc_w3', 'gc_b3', 'adaptive_range')}
    del _L0_ffn_all
    return {'x': x, 'ctx_1024': ctx_1024, 'g_xattn': g_xattn, 'g_ffn': g_ffn, 'L0_xattn_Wq': _L0_xattn_in['Wq'], 'L0_xattn_bq': _L0_xattn_in['bq'], 'L0_xattn_Wk': _L0_xattn_in['Wk'], 'L0_xattn_bk': _L0_xattn_in['bk'], 'L0_xattn_Wv': _L0_xattn_in['Wv'], 'L0_xattn_bv': _L0_xattn_in['bv'], 'L0_xattn_Wo': _L0_xattn_in['Wo'], 'L0_xattn_bo': _L0_xattn_in['bo'], 'L0_ffn_cn_w1': _L0_ffn_in['cn_w1'], 'L0_ffn_cn_b1': _L0_ffn_in['cn_b1'], 'L0_ffn_cn_w2': _L0_ffn_in['cn_w2'], 'L0_ffn_cn_b2': _L0_ffn_in['cn_b2'], 'L0_ffn_cn_w3': _L0_ffn_in['cn_w3'], 'L0_ffn_cn_b3': _L0_ffn_in['cn_b3'], 'L0_ffn_cn_w4': _L0_ffn_in['cn_w4'], 'L0_ffn_cn_b4': _L0_ffn_in['cn_b4'], 'L0_ffn_gc_w1': _L0_ffn_in['gc_w1'], 'L0_ffn_gc_b1': _L0_ffn_in['gc_b1'], 'L0_ffn_gc_w2': _L0_ffn_in['gc_w2'], 'L0_ffn_gc_b2': _L0_ffn_in['gc_b2'], 'L0_ffn_gc_w3': _L0_ffn_in['gc_w3'], 'L0_ffn_gc_b3': _L0_ffn_in['gc_b3'], 'L0_ffn_adaptive_range': _L0_ffn_in['adaptive_range']}

def reference(x, ctx_1024, g_xattn, g_ffn, L0_xattn_Wq, L0_xattn_bq, L0_xattn_Wk, L0_xattn_bk, L0_xattn_Wv, L0_xattn_bv, L0_xattn_Wo, L0_xattn_bo, L0_ffn_cn_w1, L0_ffn_cn_b1, L0_ffn_cn_w2, L0_ffn_cn_b2, L0_ffn_cn_w3, L0_ffn_cn_b3, L0_ffn_cn_w4, L0_ffn_cn_b4, L0_ffn_gc_w1, L0_ffn_gc_b1, L0_ffn_gc_w2, L0_ffn_gc_b2, L0_ffn_gc_w3, L0_ffn_gc_b3, L0_ffn_adaptive_range):
    import jax
    import jax.numpy as jnp

    def _L0_xattn_ref(query, key, value, Wq, bq, Wk, bk, Wv, bv, Wo, bo):
        import jax, jax.numpy as jnp
        import numpy as np
        HEADS = 16
        D_MODEL = 256
        D_K = D_MODEL // HEADS
        B, S, _ = query.shape

        def proj(x, W, b):
            y = x @ W.T + b
            return y.reshape(B, S, HEADS, D_K).transpose(0, 2, 1, 3)
        q = proj(query, Wq, bq)
        k = proj(key, Wk, bk)
        v = proj(value, Wv, bv)
        scores = jnp.einsum('bhqd,bhkd->bhqk', q, k) / jnp.sqrt(jnp.float32(D_K))
        p_attn = jax.nn.softmax(scores, axis=-1)
        x = jnp.einsum('bhqk,bhkd->bhqd', p_attn, v)
        x = x.transpose(0, 2, 1, 3).reshape(B, S, HEADS * D_K)
        return x @ Wo.T + bo

    def _L0_ffn_ref(x, cn_w1, cn_b1, cn_w2, cn_b2, cn_w3, cn_b3, cn_w4, cn_b4, gc_w1, gc_b1, gc_w2, gc_b2, gc_w3, gc_b3, adaptive_range):
        import jax, jax.numpy as jnp
        import numpy as np
        B, S, DIM = (4, 1024, 256)
        BASE_COUPLING = 0.1
        NUM_CYCLES = 3

        def _gelu(x):
            return jax.nn.gelu(x, approximate=False)

        def _coupling_net(h, w1, b1, w2, b2, w3, b3, w4, b4):
            h = _gelu(h @ w1 + b1)
            h = _gelu(h @ w2 + b2)
            h = _gelu(h @ w3 + b3)
            return jax.nn.sigmoid(h @ w4 + b4)

        def _global_net(h, w1, b1, w2, b2, w3, b3):
            h = _gelu(h @ w1 + b1)
            h = _gelu(h @ w2 + b2)
            return jax.nn.sigmoid(h @ w3 + b3)

        def _twist(x):
            o_r, o_i, p_r, p_i = jnp.split(x, 4, axis=-1)
            return jnp.concatenate([p_r, -p_i, -o_r, o_i], axis=-1)
        global_context = x.mean(axis=1, keepdims=True)
        gf = _global_net(global_context, gc_w1, gc_b1, gc_w2, gc_b2, gc_w3, gc_b3)
        out = x
        for _ in range(NUM_CYCLES):
            tf = _coupling_net(out, cn_w1, cn_b1, cn_w2, cn_b2, cn_w3, cn_b3, cn_w4, cn_b4)
            combined = 0.7 * gf + 0.3 * tf
            coupling = BASE_COUPLING + adaptive_range * (combined - 0.5) * 2.0
            out = out + coupling * _twist(out)
        return out
    x = x + jnp.tanh(g_xattn[0]) * _L0_xattn_ref(_layernorm(x, axis=-1), ctx_1024, ctx_1024, L0_xattn_Wq, L0_xattn_bq, L0_xattn_Wk, L0_xattn_bk, L0_xattn_Wv, L0_xattn_bv, L0_xattn_Wo, L0_xattn_bo)
    x = x + jnp.tanh(g_ffn[0]) * _L0_ffn_ref(_layernorm(x, axis=-1), L0_ffn_cn_w1, L0_ffn_cn_b1, L0_ffn_cn_w2, L0_ffn_cn_b2, L0_ffn_cn_w3, L0_ffn_cn_b3, L0_ffn_cn_w4, L0_ffn_cn_b4, L0_ffn_gc_w1, L0_ffn_gc_b1, L0_ffn_gc_w2, L0_ffn_gc_b2, L0_ffn_gc_w3, L0_ffn_gc_b3, L0_ffn_adaptive_range)
    return x

_drawn_inputs = setup_inputs


def setup_inputs(seed=0):
    import zlib

    import numpy as np

    out = dict(_drawn_inputs(seed))
    spreads = {'L0_xattn_bq': (0.0, 0.47),
     'L0_xattn_bk': (0.0, 0.8),
     'L0_xattn_bv': (0.0, 0.1),
     'L0_xattn_bo': (0.0, 0.1),
     'L0_ffn_cn_b1': (0.0, 0.8),
     'L0_ffn_cn_b2': (0.0, 0.8),
     'L0_ffn_cn_b3': (0.0, 0.619),
     'L0_ffn_gc_b1': (0.0, 0.44),
     'L0_ffn_gc_b2': (0.0, 0.452)}
    factors = {}
    for name, (base, spread) in spreads.items():
        noise = np.random.default_rng([zlib.crc32(name.encode()), seed]).standard_normal(out[name].shape)
        drawn = base * np.exp(spread * noise) if base else spread * noise
        out[name] = jnp.asarray(drawn.astype(out[name].dtype))
    for name, factor in factors.items():
        out[name] = (out[name] * factor).astype(out[name].dtype)
    return out
```

```python
import concourse.bass as bass
from concourse import mybir
from contextlib import ExitStack

FP32 = mybir.dt.float32
F32R = mybir.dt.float32r
ALU = mybir.AluOpType
ACT = mybir.ActivationFunctionType
AX = mybir.AxisListType

P = 128
B, S, D = 8, 256, 256
H = 16
DK = D // H
C = D // P
TC = S // P
HC = H // C
G = H // 4
SLOT = 32
PARTS = 4 * DK
CYCLES = 3
PAIRS = B // 2
N2 = 2 * S
EPS = 1e-5

STAGES = "ABCD"
STEPS = B + len(STAGES) - 1
LOOP = (4, 8)
LOAD_LOOP = (2, 6)


class At:

    def __init__(self, base, turn=None):
        self.base, self.turn, self.u = base, turn, base % 2

    def n(self):
        return self.base if self.turn is None else self.turn * 2 + self.base

    def back(self, n):
        return At(self.base - n, self.turn)

    def count(self, per, more):
        return per * self.base + more if self.turn is None else self.turn * (2 * per) + (per * self.base + more)

    def count_of_parity(self, per):
        k = self.base // 2 + 1
        return per * k if self.turn is None else self.turn * per + per * k


class Step:
    def __init__(self, base, turn=None):
        self.base, self.turn = base, turn

    def batch(self, stage):
        lag = STAGES.index(stage)
        if self.turn is None and not 0 <= self.base - lag < B:
            return None
        return At(self.base - lag, self.turn)


def run_steps(engine, step, loop=LOOP):
    for s in range(loop[0]):
        step(Step(s))
    with engine.Fori(0, (loop[1] - loop[0]) // 2) as turn:
        for s in range(2):
            step(Step(loop[0] + s, turn))
    for s in range(loop[1], STEPS):
        step(Step(s))


def build(nc, x, ctx_in, g_xattn, g_ffn, wq, bq, wk, bk, wv, bv, wo, bo,
          w1, b1, w2, b2, w3, b3, w4, b4, gw1, gb1, gw2, gb2, gw3, gb3, arange, out):
    with ExitStack() as stack:
        def sb(name, shape, dt=FP32):
            return stack.enter_context(nc.sbuf_tensor(name, shape, dt))

        def sem(name):
            return stack.enter_context(nc.semaphore(name))

        ident = sb("ident", [P, P])
        ones = sb("ones", [P, P])
        half_neg = sb("half_neg", [P, TC])
        eps = sb("eps", [P, TC])
        w_t = sb("w_t", [P, 4, C, D])
        w1_sb = sb("w1_sb", [P, C, D])
        w2_sb = sb("w2_sb", [P, C, P])
        w3_sb = sb("w3_sb", [P, 64])
        w4_col = sb("w4_col", [P, 2])
        w4_rep = sb("w4_rep", [P, 2, P])
        gw1_sb = sb("gw1_sb", [P, C, P])
        gw2_sb = sb("gw2_sb", [P, 64])
        gw3_col = sb("gw3_col", [64, 1])
        gw3_rep = sb("gw3_rep", [64, P])
        bqk = sb("bqk", [P, 2, C])
        bv_bc = sb("bv_bc", [P, D])
        bo_bc = sb("bo_bc", [P, D])
        thbo = sb("thbo", [P, D])
        b1_sb = sb("b1_sb", [P, C])
        b2_sb = sb("b2_sb", [P, 1])
        b3_sb = sb("b3_sb", [P, 1])
        gb1_sb = sb("gb1_sb", [P, 1])
        gb2_sb = sb("gb2_sb", [64, 1])
        scal = sb("scal", [P, 5])
        tanh_g = sb("tanh_g", [P, 2])
        half_b = sb("half_b", [P, 2])
        sign = sb("sign", [P, 1])
        gain = sb("gain", [P, 3])

        x_in = sb("x_in", [P, B, TC, D])
        c_in = sb("c_in", [P, 2, TC, D])
        stats = sb("stats", [P, TC, 6])
        mean_var = sb("mean_var", [P, TC, 2])
        var_eps = sb("var_eps", [P, TC])
        rstd = sb("rstd", [P, TC])
        xn = sb("xn", [P, TC, D])
        x_t = sb("x_t", [P, C, S])
        c_t = sb("c_t", [P, 2, C, S])
        q_hi = sb("q_hi", [P, 2, C, S], F32R)
        q_lo = sb("q_lo", [P, 2, C, S], F32R)
        k_hi = sb("k_hi", [P, 2, C, S], F32R)
        k_lo = sb("k_lo", [P, 2, C, S], F32R)
        q_st = [sb(f"q_st{u}", [P, H, S], F32R) for u in range(2)]
        k_st = [sb(f"k_st{u}", [P, H, S], F32R) for u in range(2)]
        v_sl = sb("v_sl", [P, 2, TC, H, SLOT])
        neg_max = sb("neg_max", [P, C, HC, TC])
        max_parts = sb("max_parts", [P, C, 2, HC, TC], F32R)
        max_t = [sb(f"max_t{c}", [2 * HC * TC, P], F32R) for c in range(C)]
        probs = sb("probs", [P, 2, 4, S])
        o_t = sb("o_t", [P, 2, G, S])
        rden = sb("rden", [P, TC, 2, 4])
        o_n = sb("o_n", [P, TC, D])
        o_nt = sb("o_nt", [P, C, S])
        x_b = sb("x_b", [P, TC, D])
        stats2 = sb("stats2", [P, TC, 6])
        mean_var2 = sb("mean_var2", [P, TC, 2])
        var_eps2 = sb("var_eps2", [P, TC])
        rstd2 = sb("rstd2", [P, TC])
        x2n = sb("x2n", [P, TC, D])
        x2 = sb("x2", [P, B, TC, D])
        w_raw = x2[:, 0:4, :, :]
        state = sb("state", [P, C, B, S])
        sums = sb("sums", [P, C, B])

        h1 = [x_in[:, 2 * u:2 * u + 2, :, :].rearrange("p c t d -> p c (t d)") for u in range(2)]
        twist = [x_in[:, 4 + 2 * u:6 + 2 * u, :, :].rearrange("p c t d -> p c (t d)") for u in range(2)]
        h2 = [v_sl[:, 0, u, :, :].rearrange("p h e -> p (h e)") for u in range(2)]
        tz = [v_sl[:, 1, u, :, :].rearrange("p h e -> p (h e)") for u in range(2)]
        coup = [probs[:, 0, 2 * u:2 * u + 2, :].rearrange("p a s -> p (a s)") for u in range(2)]
        h3 = [probs[:, 1, u, :] for u in range(2)]
        fin = [o_t[:, 0, 2 * u:2 * u + 2, :] for u in range(2)]
        gh1 = sb("gh1", [P, B])
        gh2 = sb("gh2", [64, B])
        gz = sb("gz", [P, B])
        base_c = sb("base_c", [P, B])

        bank = [stack.enter_context(nc.psum_tensor(f"bank{i}", [P, 512], FP32)) for i in range(8)]
        st_bank, s1_bank, pv_bank, misc = bank[0:2], bank[2:4], bank[4:6], bank[6:8]
        l1_bank, l2_bank, l3_bank, l4_bank = [bank[0:2], bank[2:4]], bank[4], bank[5], bank[6]

        names = """ident_done consts_done half_neg_done weights_in params_in small_in w_tp_ready w_t_copied tanh_done
            prep_done stacks_zeroed pool_zeroed aggr_done rstd_added rstd_done xn_done
            c_tp_ready c_t_copied x_tp_ready x_t_copied
            k_ready k_hi_done k_lo_done q_ready q_hi_done q_lo_done v_ready v_done
            s1_ready s1_maxed max_hi_done max_parts_done max_tp_ready max_t_copied
            st_ready exp_done pv_done o_t_copied o_tp_ready rden_done o_normed o_nt_ready o_nt_copied
            xb_done y_ready x2_done aggr2_done rstd2_added rstd2_done x2n_done x2_tp_ready state_ready
            l1_ready g1_done l2_ready g2_done l3_ready g3_done l4_ready tanh_z_done coup_done
            twist_done moved_done gl_ready gl_done base_done fin_tp_ready fin_done""".split()
        sem_of = {n: sem(n) for n in names}
        x_loaded = [sem(f"x_loaded{u}") for u in range(2)]
        c_loaded = [sem(f"c_loaded{u}") for u in range(2)]
        stacked = [[sem(f"stacked{u}{c}") for c in range(C)] for u in range(2)]
        max_stored = [[sem(f"max_stored{u}{c}") for c in range(C)] for u in range(2)]
        stored_u = [sem(f"stored{u}") for u in range(2)]
        (ident_done, consts_done, half_neg_done, weights_in, params_in, small_in, w_tp_ready, w_t_copied, tanh_done,
         prep_done, stacks_zeroed, pool_zeroed, aggr_done, rstd_added, rstd_done, xn_done,
         c_tp_ready, c_t_copied, x_tp_ready, x_t_copied,
         k_ready, k_hi_done, k_lo_done, q_ready, q_hi_done, q_lo_done, v_ready, v_done,
         s1_ready, s1_maxed, max_hi_done, max_parts_done, max_tp_ready, max_t_copied,
         st_ready, exp_done, pv_done, o_t_copied, o_tp_ready, rden_done, o_normed, o_nt_ready, o_nt_copied,
         xb_done, y_ready, x2_done, aggr2_done, rstd2_added, rstd2_done, x2n_done, x2_tp_ready,
         state_ready, l1_ready, g1_done, l2_ready, g2_done, l3_ready, g3_done, l4_ready, tanh_z_done, coup_done,
         twist_done, moved_done, gl_ready, gl_done, base_done, fin_tp_ready, fin_done) = [sem_of[n] for n in names]

        USES = [
            [("max1", "C", max_t_copied, 2, 2), ("o_a", "D", o_normed, 2, 1), ("o_b", "D", o_normed, 2, 2),
             ("o_nt", "D", o_nt_copied, 1, 1), ("y", "D", x2_done, 1, 1), ("x2_t", "D", state_ready, 2, 2)],
            [("c_t", "A", c_t_copied, 1, 1), ("x_t", "A", x_t_copied, 1, 1), ("k", "A", k_lo_done, 2, 2),
             ("q", "A", q_lo_done, 2, 2), ("max0", "B", max_t_copied, 2, 1), ("v", "B", v_done, 1, 1)],
        ]

        def free_bank(pe, step, use):
            m = 0 if any(u[0] == use for u in USES[0]) else 1
            order = USES[m]
            i = [u[0] for u in order].index(use)
            for back in range(1, 2 * len(order) + 1):
                name, stage, signal, per, more = order[(i - back) % len(order)]
                ago = Step(step.base - (0 if back <= i else 1 if back <= i + len(order) else 2), step.turn)
                at = ago.batch(stage)
                if at is not None:
                    pe.wait_ge(signal, at.count(per, more))
                    break
            return misc[m]

        N_PARAMS = 19
        block = stack.enter_context(nc.Block())

        @block.sync
        def _(sp):
            def load(at):
                if at.turn is not None or at.base >= 2:
                    sp.wait_ge(xn_done, at.back(2).count(1, 1))
                    sp.wait_ge(c_tp_ready, at.back(2).count(1, 1))
                b = bass.ds(at.n(), 1)
                sp.dma_start(c_in[:, at.u, :, :],
                             ctx_in[b, :, :].rearrange("b (t p) d -> p (b t) d", p=P)).then_inc(c_loaded[at.u], 16)
                sp.dma_start(x_in[:, b, :, :].rearrange("p b t d -> p (b t) d"),
                             x[b, :, :].rearrange("b (t p) d -> p (b t) d", p=P)).then_inc(x_loaded[at.u], 16)

            def stack_parts(at, c):
                if c == 0:
                    sp.wait_ge(q_lo_done, at.count(2, 2))
                elif at.turn is not None or at.base >= 2:
                    sp.wait_ge(st_ready, at.back(2).count(16, 16))
                heads = slice(c * HC, (c + 1) * HC)
                for i, (q_part, k_part) in enumerate(((q_hi, k_hi), (q_lo, k_hi), (q_hi, k_lo), (q_lo, k_lo))):
                    rows = slice(i * DK, (i + 1) * DK)
                    sp.dma_start(q_st[at.u][rows, heads, :].bitcast(FP32),
                                 q_part[:, at.u, c, :].bitcast(FP32)).then_inc(stacked[at.u][c], 16)
                    sp.dma_start(k_st[at.u][rows, heads, :].bitcast(FP32),
                                 k_part[:, at.u, c, :].bitcast(FP32)).then_inc(stacked[at.u][c], 16)
                sp.dma_start(q_st[at.u][PARTS:PARTS + 2, heads, :].bitcast(FP32),
                             k_st[0][PARTS + 2:PARTS + 4, 0:HC, :].bitcast(FP32)).then_inc(stacked[at.u][c], 16)

            def store_max(at, c):
                sp.wait_ge(max_t_copied, at.count(2, c + 1))
                sp.dma_start(q_st[at.u][PARTS:PARTS + 2, c * HC:(c + 1) * HC, :].bitcast(FP32),
                             max_t[c][:, :].bitcast(FP32)).then_inc(max_stored[at.u][c], 16)

            for i, w in enumerate((wk, wq, wv, wo)):
                sp.dma_start(w_raw[:, (1, 0, 2, 3)[i], :, :],
                             w.rearrange("(c p) i -> p c i", p=P)).then_inc(weights_in, 16)
            load(At(0))
            load(At(1))
            sp.dma_start(w1_sb[:, :, :], w1.rearrange("(c p) i -> p c i", p=P)).then_inc(params_in, 16)
            sp.dma_start(w2_sb[:, :, :], w2.rearrange("(c p) i -> p c i", p=P)).then_inc(params_in, 16)
            sp.dma_start(w3_sb[:, :], w3).then_inc(params_in, 16)
            sp.dma_start(gw1_sb[:, :, :], gw1.rearrange("(c p) i -> p c i", p=P)).then_inc(params_in, 16)
            sp.dma_start(gw2_sb[:, :], gw2).then_inc(params_in, 16)
            sp.wait_ge(stacks_zeroed, 2)
            sp.wait_ge(pool_zeroed, 3)

            def step(st):
                a, b, c = st.batch("A"), st.batch("B"), st.batch("C")
                if c:
                    store_max(c, 1)
                if a:
                    stack_parts(a, 0)
                if b:
                    store_max(b, 0)
                if st.turn is not None or st.base + 2 < B:
                    load(At(st.base + 2, st.turn))
                if a:
                    stack_parts(a, 1)

            run_steps(sp, step, LOAD_LOOP)

            with sp.Fori(0, B // 2) as turn:
                for u in range(2):
                    at = At(u, turn)
                    sp.wait_ge(fin_done, at.count(1, 1))
                    b = bass.ds(at.n(), 1)
                    sp.dma_start(out[b, :, :].rearrange("b (t p) d -> p (b t) d", p=P),
                                 fin[u]).then_inc(stored_u[u], 16)
            for u in range(2):
                sp.wait_ge(stored_u[u], 16 * (B // 2))

        @block.gpsimd
        def _(pool):
            nc.gpsimd.memset(ident[:, :], 0.0).then_inc(ident_done, 1)
            pool.wait_ge(ident_done, 1)
            nc.gpsimd.affine_select(out=ident[:, :], in_=ident[:, :], compare_op=ALU.not_equal, fill=1.0,
                                    base=0, pattern=[[-1, P]], channel_multiplier=1).then_inc(ident_done, 1)
            nc.gpsimd.memset(half_neg[:, :], -0.5).then_inc(half_neg_done, 1)
            nc.gpsimd.memset(eps[:, :], EPS).then_inc(half_neg_done, 1)
            for dst, src in (
                    (bqk[:, 0, 0:1], bq[0:P].rearrange("(h r a) -> r h a", r=DK, a=1)),
                    (bqk[:, 0, 1:2], bq[P:D].rearrange("(h r a) -> r h a", r=DK, a=1)),
                    (bqk[:, 1, 0:1], bk[0:P].rearrange("(h r a) -> r h a", r=DK, a=1)),
                    (bqk[:, 1, 1:2], bk[P:D].rearrange("(h r a) -> r h a", r=DK, a=1)),
                    (bv_bc[:, :], bv.partition_broadcast(P)),
                    (bo_bc[:, :], bo.partition_broadcast(P)),
                    (scal[:, 0:1], g_xattn.partition_broadcast(P)),
                    (scal[:, 1:2], g_ffn.partition_broadcast(P)),
                    (scal[:, 2:3], arange.partition_broadcast(P)),
                    (scal[:, 3:4], b4.partition_broadcast(P)),
                    (scal[:, 4:5], gb3.partition_broadcast(P)),
                    (b1_sb[:, 0:1], b1[0:P].rearrange("(p a) -> p a", a=1)),
                    (b1_sb[:, 1:2], b1[P:D].rearrange("(p a) -> p a", a=1)),
                    (b2_sb[:, :], b2.rearrange("(p a) -> p a", a=1)),
                    (b3_sb[0:64, :], b3.rearrange("(p a) -> p a", a=1)),
                    (b3_sb[64:P, :], b3.rearrange("(p a) -> p a", a=1)),
                    (gb1_sb[:, :], gb1.rearrange("(p a) -> p a", a=1)),
                    (gb2_sb[:, :], gb2.rearrange("(p a) -> p a", a=1)),
                    (gw3_col[:, :], gw3)):
                pool.dma_start(dst, src, allow_slow_non_contiguous=True).then_inc(small_in, 16)
            nc.gpsimd.memset(w4_col[:, :], 0.0).then_inc(pool_zeroed, 1)
            pool.wait_ge(pool_zeroed, 1)
            pool.dma_start(w4_col[0:64, 0:1], w4, allow_slow_non_contiguous=True).then_inc(small_in, 16)
            pool.dma_start(w4_col[64:P, 1:2], w4, allow_slow_non_contiguous=True).then_inc(small_in, 16)
            nc.gpsimd.memset(k_st[1][64:P, :, :].bitcast(FP32), 0.0).then_inc(pool_zeroed, 1)
            pool.wait_ge(pool_zeroed, 2)
            nc.gpsimd.memset(k_st[1][PARTS:PARTS + 2, :, :].bitcast(FP32), 1.0).then_inc(pool_zeroed, 1)

            pool.wait_ge(half_neg_done, 2)
            pool.wait_ge(pool_zeroed, 3)

            def step(st):
                a, d = st.batch("A"), st.batch("D")
                if a:
                    pool.wait_ge(aggr_done, a.count(2, 2))
                    nc.gpsimd.tensor_tensor(var_eps[:, :], mean_var[:, :, 1], eps[:, :], ALU.add).then_inc(rstd_added, 1)
                    pool.wait_ge(rstd_added, a.count(1, 1))
                    if a.turn is not None or a.base >= 1:
                        pool.wait_ge(xn_done, a.count(1, 0))
                    nc.gpsimd.tensor_tensor(rstd[:, :], var_eps[:, :], half_neg[:, :], ALU.pow).then_inc(rstd_done, 1)
                if d:
                    pool.wait_ge(prep_done, 1)
                    if d.turn is not None or d.base >= 1:
                        pool.wait_ge(x2_done, d.count(1, 0))
                    b = bass.ds(d.n(), 1)
                    for t in range(TC):
                        ins = nc.gpsimd.tensor_tensor(x_b[:, t, :], x_in[:, b, t, :].rearrange("p b d -> p (b d)"),
                                                      thbo[:, :], ALU.add)
                        ins.then_inc(xb_done, 1)
                    pool.wait_ge(aggr2_done, d.count(2, 2))
                    nc.gpsimd.tensor_tensor(var_eps2[:, :], mean_var2[:, :, 1], eps[:, :], ALU.add).then_inc(rstd2_added, 1)
                    pool.wait_ge(rstd2_added, d.count(1, 1))
                    nc.gpsimd.tensor_tensor(rstd2[:, :], var_eps2[:, :], half_neg[:, :], ALU.pow).then_inc(rstd2_done, 1)

            run_steps(pool, step)

        @block.tensor
        def _(pe):
            pe.wait_ge(ident_done, 2)
            for i, w in enumerate((1, 0, 2, 3)):
                pe.wait_ge(weights_in, 16 * 4)
                if i >= 2:
                    pe.wait_ge(w_t_copied, i - 1)
                for ci in range(C):
                    for co in range(C):
                        last = nc.tensor.transpose(misc[i % 2][:, ci * D + co * P:ci * D + (co + 1) * P],
                                                   w_raw[:, w, co, ci * P:(ci + 1) * P], ident[:, :])
                last.then_inc(w_tp_ready, 1)
            pe.wait_ge(w_t_copied, 4)

            def transposes(psum, src, ready):
                for c in range(C):
                    for t in range(TC):
                        last = nc.tensor.transpose(psum[:, c * S + t * P:c * S + (t + 1) * P],
                                                   src[:, t, c * P:(c + 1) * P], ident[:, :])
                last.then_inc(ready, 1)

            def project(psum, w, src, ready):
                for co in range(C):
                    for ci in range(C):
                        last = nc.tensor.matmul(psum[:, co * S:(co + 1) * S], w_t[:, w, ci, co * P:(co + 1) * P],
                                                src[:, ci, :], start=(ci == 0), stop=(ci == C - 1))
                last.then_inc(ready, 1)

            def scores_max_pass(b, j):
                if j % 4 == 0:
                    c = j // 4
                    pe.wait_ge(stacked[b.u][c], b.count_of_parity(16 * 9))
                for t in range(TC):
                    n = 2 * j + t
                    if b.turn is not None or b.base > 0 or n >= 2:
                        pe.wait_ge(s1_maxed, b.count(16, n - 1))
                    for i in range(2):
                        h = 2 * j + i
                        last = nc.tensor.matmul(s1_bank[t][:, i * S:(i + 1) * S],
                                                q_st[b.u][:, h, t * P:(t + 1) * P], k_st[b.u][:, h, :],
                                                start=True, stop=True)
                    last.then_inc(s1_ready, 1)

            def scores_exp_pass(c, j):
                g, t = j // 2, j % 2
                if j % 4 == 0:
                    pe.wait_ge(max_stored[c.u][j // 4], c.count_of_parity(16))
                for i in range(2):
                    n = 2 * j + i
                    if c.turn is not None or c.base > 0 or n >= 2:
                        pe.wait_ge(exp_done, c.count(16, n - 1))
                    for e in range(2):
                        h = 4 * g + 2 * i + e
                        last = nc.tensor.matmul(st_bank[i][:, e * S:(e + 1) * S],
                                                k_st[c.u][:, h, t * P:(t + 1) * P], q_st[c.u][:, h, :],
                                                start=True, stop=True)
                    last.then_inc(st_ready, 1)

            def times_values(c, j):
                g, t = j // 2, j % 2
                pe.wait_ge(exp_done, c.count(16, 2 * j + 2))
                if j == 0:
                    pe.wait_ge(v_done, c.count(1, 1))
                if t == 0 and (c.turn is not None or c.base > 0 or g >= 2):
                    pe.wait_ge(o_t_copied, c.count(4, g - 1))
                for i in range(4):
                    last = nc.tensor.matmul(pv_bank[g % 2][SLOT * i:SLOT * (i + 1), 0:S],
                                            v_sl[:, c.u, t, 4 * g + i, :], probs[:, j % 2, i, :],
                                            start=(t == 0), stop=(t == TC - 1))
                last.then_inc(pv_done, 1)

            def transpose_max(st, at, c):
                pe.wait_ge(max_parts_done, at.count(2, c + 1))
                psum = free_bank(pe, st, f"max{c}")
                nc.tensor.transpose(psum[0:2 * HC * TC, 0:P],
                                    max_parts[:, c, :, :, :].bitcast(FP32).rearrange("p a h t -> p (a h t)"),
                                    ident[:, :]).then_inc(max_tp_ready, 1)

            def transpose_outputs(st, d, half):
                pe.wait_ge(o_t_copied, d.count(4, 2 * half + 2))
                psum = free_bank(pe, st, "o_a" if half == 0 else "o_b")
                for t in range(TC):
                    for i in range(2):
                        last = nc.tensor.transpose(psum[:, (2 * t + i) * P:(2 * t + i + 1) * P],
                                                   o_t[:, d.u, 2 * half + i, t * P:(t + 1) * P], ident[:, :])
                last.then_inc(o_tp_ready, 1)

            def step(st):
                a, b, c, d = (st.batch(x) for x in STAGES)
                for j in range(8):
                    if c:
                        scores_exp_pass(c, j)
                    if j == 0 and d:
                        times_values(d, 7)
                    if j > 0 and c:
                        times_values(c, j - 1)
                    if j == 0 and a:
                        pe.wait_ge(c_loaded[a.u], a.count_of_parity(16))
                        transposes(free_bank(pe, st, "c_t"), c_in[:, a.u, :, :], c_tp_ready)
                    if b:
                        scores_max_pass(b, j)
                    if j == 0 and c:
                        transpose_max(st, c, 1)
                    if j == 1 and d:
                        transpose_outputs(st, d, 0)
                    if j == 1 and a:
                        pe.wait_ge(xn_done, a.count(1, 1))
                        transposes(free_bank(pe, st, "x_t"), xn, x_tp_ready)
                    if j == 2:
                        if a:
                            pe.wait_ge(c_t_copied, a.count(1, 1))
                            project(free_bank(pe, st, "k"), 1, c_t[:, a.u, :, :], k_ready)
                        if d:
                            transpose_outputs(st, d, 1)
                    if j == 3:
                        if a:
                            pe.wait_ge(x_t_copied, a.count(1, 1))
                            project(free_bank(pe, st, "q"), 0, x_t, q_ready)
                        if d:
                            pe.wait_ge(o_normed, d.count(2, 2))
                            transposes(free_bank(pe, st, "o_nt"), o_n, o_nt_ready)
                    if j == 4 and d:
                        pe.wait_ge(o_nt_copied, d.count(1, 1))
                        psum = free_bank(pe, st, "y")
                        for t in range(TC):
                            for ci in range(C):
                                last = nc.tensor.matmul(psum[:, t * D:(t + 1) * D], o_nt[:, ci, t * P:(t + 1) * P],
                                                        w_t[:, 3, ci, :], start=(ci == 0), stop=(ci == C - 1))
                        last.then_inc(y_ready, 1)
                    if j == 5 and b:
                        transpose_max(st, b, 0)
                    if j == 6 and b:
                        pe.wait_ge(c_t_copied, b.count(1, 1))
                        psum = free_bank(pe, st, "v")
                        for t in range(TC):
                            for ci in range(C):
                                last = nc.tensor.matmul(psum[:, t * D:(t + 1) * D], c_t[:, b.u, ci, t * P:(t + 1) * P],
                                                        w_t[:, 2, ci, :], start=(ci == 0), stop=(ci == C - 1))
                        last.then_inc(v_ready, 1)
                    if j == 7 and d:
                        pe.wait_ge(x2n_done, d.count(1, 1))
                        transposes(free_bank(pe, st, "x2_t"), x2n, x2_tp_ready)

            run_steps(pe, step)

            def layer1(n, co):
                p = n % PAIRS
                if n >= PAIRS:
                    pe.wait_ge(moved_done, 2 * (n - PAIRS) + 2)
                if n >= 2:
                    pe.wait_ge(g1_done, 2 * (n - 2) + co + 1)
                for ci in range(C):
                    last = nc.tensor.matmul(l1_bank[n % 2][co][:, :], w1_sb[:, ci, co * P:(co + 1) * P],
                                            state[:, ci, 2 * p:2 * p + 2, :].rearrange("p b s -> p (b s)"),
                                            start=(ci == 0), stop=(ci == C - 1))
                last.then_inc(l1_ready, 1)

            def layer2(n):
                pe.wait_ge(g1_done, 2 * n + 2)
                if n >= 1:
                    pe.wait_ge(g2_done, n)
                for ci in range(C):
                    last = nc.tensor.matmul(l2_bank[:, :], w2_sb[:, ci, :], h1[n % 2][:, ci, :],
                                            start=(ci == 0), stop=(ci == C - 1))
                last.then_inc(l2_ready, 1)

            def layer3(n):
                pe.wait_ge(g2_done, n + 1)
                if n >= 1:
                    pe.wait_ge(g3_done, n)
                for half in range(2):
                    last = nc.tensor.matmul(l3_bank[64 * half:64 * (half + 1), 0:S], w3_sb[:, :],
                                            h2[n % 2][:, half * S:(half + 1) * S], start=True, stop=True)
                last.then_inc(l3_ready, 1)

            def layer4(n):
                pe.wait_ge(g3_done, n + 1)
                if n >= 1:
                    pe.wait_ge(tanh_z_done, n)
                for half in range(2):
                    last = nc.tensor.matmul(l4_bank[:, half * S:(half + 1) * S], w4_rep[:, half, :], h3[n % 2],
                                            start=True, stop=True)
                last.then_inc(l4_ready, 1)

            def ffn_step(n):
                if n < CYCLES * PAIRS:
                    layer1(n, 0)
                if 0 <= n - 2:
                    layer3(n - 2)
                if n < CYCLES * PAIRS:
                    layer1(n, 1)
                if 0 <= n - 2:
                    layer4(n - 2)
                if 0 <= n - 1 < CYCLES * PAIRS:
                    layer2(n - 1)

            pe.wait_ge(state_ready, 2 * B)
            ffn_step(0)
            pe.wait_ge(params_in, 16 * 5)
            for ci in range(C):
                last = nc.tensor.matmul(l4_bank[:, 0:B], gw1_sb[:, ci, :], sums[:, ci, :],
                                        start=(ci == 0), stop=(ci == C - 1))
            last.then_inc(gl_ready, 1)
            pe.wait_ge(gl_done, 1)
            nc.tensor.matmul(l4_bank[0:64, 64:64 + B], gw2_sb[:, :], gh1[:, :], start=True, stop=True).then_inc(gl_ready, 1)
            ffn_step(1)
            pe.wait_ge(gl_done, 2)
            nc.tensor.matmul(l4_bank[:, 128:128 + B], gw3_rep[:, :], gh2[:, :], start=True, stop=True).then_inc(gl_ready, 1)
            pe.wait_ge(gl_done, 3)
            for n in range(2, CYCLES * PAIRS + 2):
                ffn_step(n)

            for b in range(B):
                pe.wait_ge(moved_done, 2 * ((CYCLES - 1) * PAIRS + b // 2) + 2)
                if b >= 2:
                    pe.wait_ge(fin_done, b - 1)
                else:
                    pe.wait_ge(g1_done, 2 * CYCLES * PAIRS)
                for t in range(TC):
                    for ci in range(C):
                        last = nc.tensor.transpose(l1_bank[b % 2][0][:, t * D + ci * P:t * D + (ci + 1) * P],
                                                   state[:, ci, b, t * P:(t + 1) * P], ident[:, :])
                last.then_inc(fin_tp_ready, 1)

        @block.scalar
        def _(act):
            for i, w in enumerate((1, 0, 2, 3)):
                act.wait_ge(w_tp_ready, i + 1)
                src = misc[i % 2][:, :].rearrange("p (a n) -> p a n", a=2 * C)
                dst = w_t[:, w, :, :].rearrange("p a (c n) -> p (a c) n", c=C)
                if w < 2:
                    src = src.rearrange("p a (h r) -> p a h r", r=DK)
                    dst = dst.rearrange("p a (r h) -> p a h r", r=DK)
                nc.scalar.copy(dst, src).then_inc(w_t_copied, 1)
            act.wait_ge(small_in, 16 * 21)
            nc.scalar.activation(tanh_g[:, :], scal[:, 0:2], ACT.Tanh).then_inc(tanh_done, 1)

            def project_hi(at, i, dst, ready, done, psum):
                act.wait_ge(ready, at.count(1, 1))
                for c in range(C):
                    nc.scalar.activation(dst[:, at.u, c, :], psum[:, c * S:(c + 1) * S], ACT.Identity,
                                         bias=bqk[:, i, c:c + 1]).then_inc(done, 1)

            def copy_max(at, c, m):
                act.wait_ge(max_tp_ready, at.count(2, c + 1))
                if at.turn is not None or at.base >= 1:
                    last = at.back(1)
                    act.wait_ge(max_stored[last.u][c], last.count_of_parity(16))
                nc.scalar.copy(max_t[c][:, :], misc[m][0:2 * HC * TC, 0:P]).then_inc(max_t_copied, 1)

            def copy_outputs(at, g):
                act.wait_ge(pv_done, at.count(8, 2 * g + 2))
                nc.scalar.copy(o_t[:, at.u, g, :], pv_bank[g % 2][:, 0:S]).then_inc(o_t_copied, 1)

            def step(st):
                a, b, c, d = (st.batch(x) for x in STAGES)
                for j in range(8):
                    if c:
                        for i in range(2):
                            act.wait_ge(st_ready, c.count(16, 2 * j + i + 1))
                            if i == 0 and (c.turn is not None or c.base > 0 or j >= 2):
                                act.wait_ge(pv_done, c.count(8, j - 1))
                            nc.scalar.activation(probs[:, j % 2, 2 * i:2 * i + 2, :].rearrange("p e s -> p (e s)"),
                                                 st_bank[i][:, :], ACT.Exp, scale=DK ** -0.5).then_inc(exp_done, 1)
                    if j == 0 and d:
                        copy_outputs(d, 3)
                    if j == 0 and a:
                        act.wait_ge(c_tp_ready, a.count(1, 1))
                        nc.scalar.copy(c_t[:, a.u, :, :].rearrange("p c s -> p (c s)"), misc[1][:, :]).then_inc(c_t_copied, 1)
                    if j == 0 and c:
                        copy_max(c, 1, 0)
                    if j == 1 and a:
                        act.wait_ge(x_tp_ready, a.count(1, 1))
                        nc.scalar.copy(x_t[:, :, :].rearrange("p c s -> p (c s)"), misc[1][:, :]).then_inc(x_t_copied, 1)
                    if j == 2 and c:
                        copy_outputs(c, 0)
                    if j == 2 and a:
                        project_hi(a, 1, k_hi, k_ready, k_hi_done, misc[1])
                    if j == 3 and a:
                        project_hi(a, 0, q_hi, q_ready, q_hi_done, misc[1])
                    if j == 3 and d:
                        act.wait_ge(o_nt_ready, d.count(1, 1))
                        nc.scalar.copy(o_nt[:, :, :].rearrange("p c s -> p (c s)"), misc[0][:, :]).then_inc(o_nt_copied, 1)
                    if j == 4 and c:
                        copy_outputs(c, 1)
                    if j == 5 and b:
                        copy_max(b, 0, 1)
                    if j == 6 and c:
                        copy_outputs(c, 2)
                    if j == 7 and d:
                        act.wait_ge(x2_tp_ready, d.count(1, 1))
                        for ci in range(C):
                            nc.scalar.activation(state[:, ci, bass.ds(d.n(), 1), :].rearrange("p b s -> p (b s)"),
                                                 misc[0][:, ci * S:(ci + 1) * S], ACT.Identity,
                                                 accum_out=sums[:, ci, bass.ds(d.n(), 1)]).then_inc(state_ready, 1)

            run_steps(act, step)

            def gelu1(n):
                for co in range(C):
                    act.wait_ge(l1_ready, 2 * n + co + 1)
                    if co == 0 and n >= 2:
                        act.wait_ge(l2_ready, n - 1)
                    nc.scalar.activation(h1[n % 2][:, co, :], l1_bank[n % 2][co][:, :], ACT.Gelu,
                                         bias=b1_sb[:, co:co + 1]).then_inc(g1_done, 1)

            def gelu2(n):
                act.wait_ge(l2_ready, n + 1)
                if n >= 2:
                    act.wait_ge(l3_ready, n - 1)
                nc.scalar.activation(h2[n % 2], l2_bank[:, :], ACT.Gelu, bias=b2_sb[:, :]).then_inc(g2_done, 1)

            def gelu3(n):
                act.wait_ge(l3_ready, n + 1)
                if n >= 2:
                    act.wait_ge(l4_ready, n - 1)
                nc.scalar.activation(h3[n % 2], l3_bank[:, 0:S], ACT.Gelu, bias=b3_sb[:, :]).then_inc(g3_done, 1)

            def tanh_z(n):
                act.wait_ge(l4_ready, n + 1)
                if n >= 2:
                    act.wait_ge(coup_done, 2 * (n - 1))
                nc.scalar.activation(tz[n % 2], l4_bank[:, :], ACT.Tanh, bias=half_b[:, 0:1], scale=0.5).then_inc(tanh_z_done, 1)

            act.wait_ge(prep_done, 1)
            act.wait_ge(gl_ready, 1)
            nc.scalar.activation(gh1[:, :], l4_bank[:, 0:B], ACT.Gelu, bias=gb1_sb[:, :], scale=1.0 / S).then_inc(gl_done, 1)
            gelu1(0)
            act.wait_ge(gl_ready, 2)
            nc.scalar.activation(gh2[:, :], l4_bank[0:64, 64:64 + B], ACT.Gelu, bias=gb2_sb[:, :]).then_inc(gl_done, 1)
            gelu1(1)
            gelu2(0)
            act.wait_ge(gl_ready, 3)
            nc.scalar.activation(gz[:, :], l4_bank[:, 128:128 + B], ACT.Tanh, bias=half_b[:, 1:2], scale=0.5).then_inc(gl_done, 1)
            for n in range(2, CYCLES * PAIRS + 2):
                gelu3(n - 2)
                if n < CYCLES * PAIRS:
                    gelu1(n)
                tanh_z(n - 2)
                if n - 1 < CYCLES * PAIRS:
                    gelu2(n - 1)

        @block.vector
        def _(dve):
            nc.vector.memset(ones[:, :], 1.0).then_inc(consts_done, 1)
            nc.vector.memset(v_sl[:, :, :, :, DK:SLOT].rearrange("p u t h e -> p (u t h) e"), 0.0).then_inc(consts_done, 1)
            nc.vector.memset(k_st[0][64:P, :, :].bitcast(FP32), 0.0).then_inc(stacks_zeroed, 1)
            nc.vector.memset(q_st[0][64:P, :, :].bitcast(FP32), 0.0).then_inc(consts_done, 1)
            nc.vector.memset(q_st[1][64:P, :, :].bitcast(FP32), 0.0).then_inc(consts_done, 1)
            dve.wait_ge(stacks_zeroed, 1)
            nc.vector.memset(k_st[0][PARTS:PARTS + 2, :, :].bitcast(FP32), 1.0).then_inc(stacks_zeroed, 1)
            dve.wait_ge(consts_done, 2)
            nc.vector.memset(v_sl[:, :, :, :, DK:DK + 1].rearrange("p u t h e -> p (u t h) e"), 1.0).then_inc(consts_done, 1)

            def prepare():
                dve.wait_ge(small_in, 16 * 21)
                for half in range(2):
                    nc.vector.tensor_scalar(w4_rep[:, half, :], ones[:, :], w4_col[:, half:half + 1], None, ALU.mult)
                nc.vector.tensor_scalar(gw3_rep[:, :], ones[0:64, :], gw3_col[:, :], None, ALU.mult)
                nc.vector.tensor_scalar(half_b[:, :], scal[:, 3:5], 0.5, None, ALU.mult)
                nc.vector.tensor_scalar(gain[:, 0:1], scal[:, 2:3], 0.3, None, ALU.mult)
                nc.vector.tensor_scalar(gain[:, 1:2], scal[:, 2:3], 0.7, None, ALU.mult)
                nc.vector.memset(sign[0:64, :], 1.0)
                nc.vector.memset(sign[64:P, :], -1.0)
                dve.wait_ge(tanh_done, 1)
                nc.vector.tensor_scalar(thbo[:, :], bo_bc[:, :], tanh_g[:, 0:1], None, ALU.mult).then_inc(prep_done, 1)

            def max_of(b, j):
                for t in range(TC):
                    dve.wait_ge(s1_ready, b.count(16, 2 * j + t + 1))
                    nc.vector.tensor_reduce(neg_max[:, j // 4, 2 * (j % 4):2 * (j % 4) + 2, t],
                                            s1_bank[t][:, :].rearrange("p (e s) -> p e s", e=2),
                                            AX.X, ALU.max, negate=True).then_inc(s1_maxed, 1)

            def split_max(at, c):
                dve.wait_ge(s1_maxed, at.count(16, 8 * (c + 1)))
                if at.turn is not None or at.base >= 1:
                    dve.wait_ge(max_tp_ready, at.count(2, c - 1))
                nm = neg_max[:, c, :, :].rearrange("p h t -> p (h t)")
                hi, lo = (max_parts[:, c, i, :, :].rearrange("p h t -> p (h t)") for i in range(2))
                nc.vector.tensor_copy(hi, nm).then_inc(max_hi_done, 1)
                dve.wait_ge(max_hi_done, at.count(2, c + 1))
                nc.vector.tensor_tensor(lo, nm, hi.bitcast(FP32), ALU.subtract).then_inc(max_parts_done, 1)

            def project_lo(at, i, hi, lo, hi_done, done):
                dve.wait_ge(hi_done, at.count(2, 2))
                for c in range(C):
                    nc.vector.scalar_tensor_tensor(lo[:, at.u, c, :], misc[1][:, c * S:(c + 1) * S], bqk[:, i, c:c + 1],
                                                   hi[:, at.u, c, :].bitcast(FP32), ALU.add, ALU.subtract).then_inc(done, 1)

            def norm_outputs(d, half):
                dve.wait_ge(o_tp_ready, d.count(2, half + 1))
                src = misc[0][:, :].rearrange("p (t h e) -> p t h e", t=TC, e=SLOT)
                rd = rden[:, :, :, :].rearrange("p t g i -> p t (g i)")
                nc.vector.reciprocal(rd, src[:, :, :, DK]).then_inc(rden_done, 1)
                dve.wait_ge(rden_done, d.count(2, half + 1))
                if half == 0 and (d.turn is not None or d.base >= 1):
                    dve.wait_ge(o_nt_ready, d.count(1, 0))
                nc.vector.tensor_tensor(o_n[:, :, half * P:(half + 1) * P].rearrange("p t (h e) -> p t h e", e=DK),
                                        src[:, :, :, 0:DK], rd.unsqueeze(3).to_broadcast([P, TC, HC, DK]),
                                        ALU.mult).then_inc(o_normed, 1)

            def step(st):
                a, b, c, d = (st.batch(x) for x in STAGES)
                for j in range(8):
                    if j == 0 and c:
                        split_max(c, 1)
                    if j == 4 and b:
                        split_max(b, 0)
                    if b:
                        max_of(b, j)
                    if j == 0 and a:
                        dve.wait_ge(x_loaded[a.u], a.count_of_parity(16))
                        for t in range(TC):
                            nc.vector.bn_stats(stats[:, t, :], x_in[:, bass.ds(a.n(), 1), t, :].rearrange("p b d -> p (b d)"))
                        dve.drain()
                        for t in range(TC):
                            nc.vector.bn_aggr(mean_var[:, t, :], stats[:, t, :]).then_inc(aggr_done, 1)
                    if j == 1 and a:
                        dve.wait_ge(rstd_done, a.count(1, 1))
                        if a.turn is not None or a.base >= 1:
                            dve.wait_ge(x_tp_ready, a.count(1, 0))
                        for t in range(TC):
                            last = nc.vector.tensor_scalar(xn[:, t, :], x_in[:, bass.ds(a.n(), 1), t, :].rearrange("p b d -> p (b d)"),
                                                           mean_var[:, t, 0:1], rstd[:, t:t + 1], ALU.subtract, ALU.mult)
                        last.then_inc(xn_done, 1)
                    if j == 1 and d:
                        norm_outputs(d, 0)
                    if j == 2 and d:
                        norm_outputs(d, 1)
                    if j == 2 and a:
                        project_lo(a, 1, k_hi, k_lo, k_hi_done, k_lo_done)
                    if j == 3 and a:
                        project_lo(a, 0, q_hi, q_lo, q_hi_done, q_lo_done)
                    if j == 5 and d:
                        dve.wait_ge(y_ready, d.count(1, 1))
                        dve.wait_ge(xb_done, d.count(2, 2))
                        nc.vector.scalar_tensor_tensor(x2[:, bass.ds(d.n(), 1), :, :].rearrange("p b t d -> p (b t d)"),
                                                       misc[0][:, :], tanh_g[:, 0:1], x_b[:, :, :].rearrange("p t d -> p (t d)"),
                                                       ALU.mult, ALU.add).then_inc(x2_done, 1)
                        dve.drain()
                        for t in range(TC):
                            nc.vector.bn_stats(stats2[:, t, :], x2[:, bass.ds(d.n(), 1), t, :].rearrange("p b d -> p (b d)"))
                        dve.drain()
                        for t in range(TC):
                            nc.vector.bn_aggr(mean_var2[:, t, :], stats2[:, t, :]).then_inc(aggr2_done, 1)
                    if j == 6 and b:
                        dve.wait_ge(v_ready, b.count(1, 1))
                        if b.base == 0:
                            dve.wait_ge(consts_done, 5)
                        nc.vector.tensor_tensor(v_sl[:, b.u, :, :, 0:DK], misc[1][:, :].rearrange("p (t h e) -> p t h e", t=TC, e=DK),
                                                bv_bc[:, :].rearrange("p (h e) -> p h e", e=DK).unsqueeze(1).to_broadcast([P, TC, H, DK]),
                                                ALU.add).then_inc(v_done, 1)
                    if j == 6 and d:
                        dve.wait_ge(rstd2_done, d.count(1, 1))
                        for t in range(TC):
                            last = nc.vector.tensor_scalar(x2n[:, t, :], x2[:, bass.ds(d.n(), 1), t, :].rearrange("p b d -> p (b d)"),
                                                           mean_var2[:, t, 0:1], rstd2[:, t:t + 1], ALU.subtract, ALU.mult)
                        last.then_inc(x2n_done, 1)

            prepare()
            run_steps(dve, step)

            dve.wait_ge(gl_done, 3)
            nc.vector.tensor_scalar(base_c[:, :], gz[:, :], gain[:, 1:2], 0.1, ALU.mult, ALU.add).then_inc(base_done, 1)
            dve.wait_ge(base_done, 1)
            for n in range(CYCLES * PAIRS):
                p = n % PAIRS
                dve.wait_ge(tanh_z_done, n + 1)
                for half in range(2):
                    nc.vector.tensor_scalar(coup[n % 2][:, half * S:(half + 1) * S], tz[n % 2][:, half * S:(half + 1) * S],
                                            gain[:, 0:1], base_c[:, 2 * p + half:2 * p + half + 1],
                                            ALU.mult, ALU.add).then_inc(coup_done, 1)
                dve.wait_ge(coup_done, 2 * n + 2)
                half_state = [state[:, ci, 2 * p:2 * p + 2, :].rearrange("p b s -> p (b s)") for ci in range(C)]
                for ci in range(C):
                    nc.vector.scalar_tensor_tensor(twist[n % 2][:, ci, :], half_state[1 - ci], sign[:, :], coup[n % 2],
                                                   ALU.mult, ALU.mult).then_inc(twist_done, 1)
                for ci in range(C):
                    dve.wait_ge(twist_done, 2 * n + 2)
                    nc.vector.tensor_tensor(half_state[ci], half_state[ci], twist[n % 2][:, ci, :],
                                            ALU.add if ci == 0 else ALU.subtract).then_inc(moved_done, 1)
            for b in range(B):
                dve.wait_ge(fin_tp_ready, b + 1)
                if b >= 2:
                    dve.wait_ge(stored_u[b % 2], 16 * (b // 2))
                nc.vector.scalar_tensor_tensor(fin[b % 2].rearrange("p t d -> p (t d)"), l1_bank[b % 2][0][:, :], tanh_g[:, 1:2],
                                               x2[:, b, :, :].rearrange("p t d -> p (t d)"), ALU.mult, ALU.add).then_inc(fin_done, 1)


_INS = ['x', 'ctx_1024', 'g_xattn', 'g_ffn', 'L0_xattn_Wq', 'L0_xattn_bq', 'L0_xattn_Wk', 'L0_xattn_bk',
        'L0_xattn_Wv', 'L0_xattn_bv', 'L0_xattn_Wo', 'L0_xattn_bo',
        'L0_ffn_cn_w1', 'L0_ffn_cn_b1', 'L0_ffn_cn_w2', 'L0_ffn_cn_b2', 'L0_ffn_cn_w3', 'L0_ffn_cn_b3',
        'L0_ffn_cn_w4', 'L0_ffn_cn_b4', 'L0_ffn_gc_w1', 'L0_ffn_gc_b1', 'L0_ffn_gc_w2', 'L0_ffn_gc_b2',
        'L0_ffn_gc_w3', 'L0_ffn_gc_b3', 'L0_ffn_adaptive_range']


def kernel(**inputs):
    import numpy as _np
    import concourse.bacc as _bacc
    from concourse import mybir as _mybir
    from concourse.bass_utils import run_bass_kernel_spmd as _run

    nc = _bacc.Bacc("TRN2", target_bir_lowering=False, num_devices=1)
    arrays, args = {}, []
    for name in _INS:
        a = _np.ascontiguousarray(inputs[name])
        arrays[f"in_{name}_dram"] = a
        args.append(nc.dram_tensor(f"in_{name}_dram", a.shape, _mybir.dt.from_np(a.dtype), kind="ExternalInput").ap())
    args.append(nc.dram_tensor("out_0_dram", (B, S, D), _mybir.dt.float32, kind="ExternalOutput").ap())
    build(nc, *args)
    r = _run(nc, [arrays], core_ids=[0])
    return r.results[0]["out_0_dram"]
```

```python
import concourse.bass as bass
from concourse import mybir
from contextlib import ExitStack

FP32 = mybir.dt.float32
F32R = mybir.dt.float32r
ALU = mybir.AluOpType
ACT = mybir.ActivationFunctionType
AX = mybir.AxisListType

P = 128
B, S, D = 8, 256, 256
H = 16
DK = D // H
C = D // P
TC = S // P
HC = H // C
G = H // 4
SLOT = 32
PARTS = 4 * DK
CYCLES = 3
PAIRS = B // 2
N2 = 2 * S
EPS = 1e-5

STAGES = "ABCD"
STEPS = B + len(STAGES) - 1
LOOP = (4, 8)
LOAD_LOOP = (2, 6)


class At:

    def __init__(self, base, turn=None):
        self.base, self.turn, self.u = base, turn, base % 2

    def n(self):
        return self.base if self.turn is None else self.turn * 2 + self.base

    def back(self, n):
        return At(self.base - n, self.turn)

    def count(self, per, more):
        return per * self.base + more if self.turn is None else self.turn * (2 * per) + (per * self.base + more)

    def count_of_parity(self, per):
        k = self.base // 2 + 1
        return per * k if self.turn is None else self.turn * per + per * k


class Step:
    def __init__(self, base, turn=None):
        self.base, self.turn = base, turn

    def batch(self, stage):
        lag = STAGES.index(stage)
        if self.turn is None and not 0 <= self.base - lag < B:
            return None
        return At(self.base - lag, self.turn)


def run_steps(engine, step, loop=LOOP):
    for s in range(loop[0]):
        step(Step(s))
    with engine.Fori(0, (loop[1] - loop[0]) // 2) as turn:
        for s in range(2):
            step(Step(loop[0] + s, turn))
    for s in range(loop[1], STEPS):
        step(Step(s))


def build(nc, x, ctx_in, g_xattn, g_ffn, wq, bq, wk, bk, wv, bv, wo, bo,
          w1, b1, w2, b2, w3, b3, w4, b4, gw1, gb1, gw2, gb2, gw3, gb3, arange, out):
    with ExitStack() as stack:
        def sb(name, shape, dt=FP32):
            return stack.enter_context(nc.sbuf_tensor(name, shape, dt))

        def sem(name):
            return stack.enter_context(nc.semaphore(name))

        ident = sb("ident", [P, P])
        ones = sb("ones", [P, P])
        half_neg = sb("half_neg", [P, TC])
        eps = sb("eps", [P, TC])
        w_t = sb("w_t", [P, 4, C, D])
        w1_sb = sb("w1_sb", [P, C, D])
        w2_sb = sb("w2_sb", [P, C, P])
        w3_sb = sb("w3_sb", [P, 64])
        w4_col = sb("w4_col", [P, 2])
        w4_rep = sb("w4_rep", [P, 2, P])
        gw1_sb = sb("gw1_sb", [P, C, P])
        gw2_sb = sb("gw2_sb", [P, 64])
        gw3_col = sb("gw3_col", [64, 1])
        gw3_rep = sb("gw3_rep", [64, P])
        bqk = sb("bqk", [P, 2, C])
        bv_bc = sb("bv_bc", [P, D])
        bo_bc = sb("bo_bc", [P, D])
        thbo = sb("thbo", [P, D])
        b1_sb = sb("b1_sb", [P, C])
        b2_sb = sb("b2_sb", [P, 1])
        b3_sb = sb("b3_sb", [P, 1])
        gb1_sb = sb("gb1_sb", [P, 1])
        gb2_sb = sb("gb2_sb", [64, 1])
        scal = sb("scal", [P, 5])
        tanh_g = sb("tanh_g", [P, 2])
        half_b = sb("half_b", [P, 2])
        sign = sb("sign", [P, 1])
        gain = sb("gain", [P, 3])

        x_in = sb("x_in", [P, B, TC, D])
        c_in = sb("c_in", [P, 2, TC, D])
        stats = sb("stats", [P, TC, 6])
        mean_var = sb("mean_var", [P, TC, 2])
        var_eps = sb("var_eps", [P, TC])
        rstd = sb("rstd", [P, TC])
        xn = sb("xn", [P, TC, D])
        x_t = sb("x_t", [P, C, S])
        c_t = sb("c_t", [P, 2, C, S])
        q_hi = sb("q_hi", [P, 2, C, S], F32R)
        q_lo = sb("q_lo", [P, 2, C, S], F32R)
        k_hi = sb("k_hi", [P, 2, C, S], F32R)
        k_lo = sb("k_lo", [P, 2, C, S], F32R)
        q_st = [sb(f"q_st{u}", [P, H, S], F32R) for u in range(2)]
        k_st = [sb(f"k_st{u}", [P, H, S], F32R) for u in range(2)]
        v_sl = sb("v_sl", [P, 2, TC, H, SLOT])
        neg_max = sb("neg_max", [P, C, HC, TC])
        max_parts = sb("max_parts", [P, C, 2, HC, TC], F32R)
        max_t = [sb(f"max_t{c}", [2 * HC * TC, P], F32R) for c in range(C)]
        probs = sb("probs", [P, 2, 4, S])
        o_t = sb("o_t", [P, 2, G, S])
        rden = sb("rden", [P, TC, 2, 4])
        o_n = sb("o_n", [P, TC, D])
        o_nt = sb("o_nt", [P, C, S])
        x_b = sb("x_b", [P, TC, D])
        stats2 = sb("stats2", [P, TC, 6])
        mean_var2 = sb("mean_var2", [P, TC, 2])
        var_eps2 = sb("var_eps2", [P, TC])
        rstd2 = sb("rstd2", [P, TC])
        x2n = sb("x2n", [P, TC, D])
        x2 = sb("x2", [P, B, TC, D])
        w_raw = x2[:, 0:4, :, :]
        state = sb("state", [P, C, B, S])
        sums = sb("sums", [P, C, B])

        h1 = [x_in[:, 2 * u:2 * u + 2, :, :].rearrange("p c t d -> p c (t d)") for u in range(2)]
        twist = [x_in[:, 4 + 2 * u:6 + 2 * u, :, :].rearrange("p c t d -> p c (t d)") for u in range(2)]
        h2 = [v_sl[:, 0, u, :, :].rearrange("p h e -> p (h e)") for u in range(2)]
        tz = [v_sl[:, 1, u, :, :].rearrange("p h e -> p (h e)") for u in range(2)]
        coup = [probs[:, 0, 2 * u:2 * u + 2, :].rearrange("p a s -> p (a s)") for u in range(2)]
        h3 = [probs[:, 1, u, :] for u in range(2)]
        fin = [o_t[:, 0, 2 * u:2 * u + 2, :] for u in range(2)]
        gh1 = sb("gh1", [P, B])
        gh2 = sb("gh2", [64, B])
        gz = sb("gz", [P, B])
        base_c = sb("base_c", [P, B])

        bank = [stack.enter_context(nc.psum_tensor(f"bank{i}", [P, 512], FP32)) for i in range(8)]
        st_bank, s1_bank, pv_bank, misc = bank[0:2], bank[2:4], bank[4:6], bank[6:8]
        l1_bank, l2_bank, l3_bank, l4_bank = [bank[0:2], bank[2:4]], bank[4], bank[5], bank[6]

        names = """ident_done half_neg_done params_in gates_in small_in bias_in ones_stored w_tp_ready w_t_copied tanh_done
            prep_done gates_ready k0_zeroed k1_zeroed q0_zeroed q1_zeroed w4_zeroed ones_done v_zeroed v_ones aggr_done rstd_added rstd_done xn_done
            c_tp_ready c_t_copied x_tp_ready x_t_copied
            k_ready k_hi_done k_lo_done q_ready q_hi_done q_lo_done v_ready v_done
            s1_ready s1_maxed max_hi_done max_parts_done max_tp_ready max_t_copied
            st_ready exp_done pv_done o_t_copied o_tp_ready rden_done o_normed o_nt_ready o_nt_copied
            xb_done y_ready x2_done aggr2_done rstd2_added rstd2_done x2n_done x2_tp_ready state_ready
            l1_ready g1_done l2_ready g2_done l3_ready g3_done l4_ready tanh_z_done coup_done
            twist_done moved_done gl_ready gl_done base_done fin_tp_ready fin_done""".split()
        sem_of = {n: sem(n) for n in names}
        x_loaded = [sem(f"x_loaded{u}") for u in range(2)]
        c_loaded = [sem(f"c_loaded{u}") for u in range(2)]
        stacked = [[sem(f"stacked{u}{c}") for c in range(C)] for u in range(2)]
        max_stored = [[sem(f"max_stored{u}{c}") for c in range(C)] for u in range(2)]
        weight_in = [sem(f"weight_in{i}") for i in range(4)]
        stored_u = [sem(f"stored{u}") for u in range(2)]
        (ident_done, half_neg_done, params_in, gates_in, small_in, bias_in, ones_stored, w_tp_ready, w_t_copied, tanh_done,
         prep_done, gates_ready, k0_zeroed, k1_zeroed, q0_zeroed, q1_zeroed, w4_zeroed, ones_done, v_zeroed, v_ones, aggr_done, rstd_added, rstd_done, xn_done,
         c_tp_ready, c_t_copied, x_tp_ready, x_t_copied,
         k_ready, k_hi_done, k_lo_done, q_ready, q_hi_done, q_lo_done, v_ready, v_done,
         s1_ready, s1_maxed, max_hi_done, max_parts_done, max_tp_ready, max_t_copied,
         st_ready, exp_done, pv_done, o_t_copied, o_tp_ready, rden_done, o_normed, o_nt_ready, o_nt_copied,
         xb_done, y_ready, x2_done, aggr2_done, rstd2_added, rstd2_done, x2n_done, x2_tp_ready,
         state_ready, l1_ready, g1_done, l2_ready, g2_done, l3_ready, g3_done, l4_ready, tanh_z_done, coup_done,
         twist_done, moved_done, gl_ready, gl_done, base_done, fin_tp_ready, fin_done) = [sem_of[n] for n in names]

        USES = [
            [("max1", "C", max_t_copied, 2, 2), ("o_a", "D", o_normed, 2, 1), ("o_b", "D", o_normed, 2, 2),
             ("o_nt", "D", o_nt_copied, 1, 1), ("y", "D", x2_done, 1, 1), ("x2_t", "D", state_ready, 2, 2)],
            [("c_t", "A", c_t_copied, 1, 1), ("k", "A", k_lo_done, 2, 2), ("x_t", "A", x_t_copied, 1, 1),
             ("q", "A", q_lo_done, 2, 2), ("max0", "B", max_t_copied, 2, 1), ("v", "B", v_done, 1, 1)],
        ]

        def free_bank(pe, step, use):
            m = 0 if any(u[0] == use for u in USES[0]) else 1
            order = USES[m]
            i = [u[0] for u in order].index(use)
            for back in range(1, 2 * len(order) + 1):
                name, stage, signal, per, more = order[(i - back) % len(order)]
                ago = Step(step.base - (0 if back <= i else 1 if back <= i + len(order) else 2), step.turn)
                at = ago.batch(stage)
                if at is not None:
                    pe.wait_ge(signal, at.count(per, more))
                    break
            return misc[m]

        def query_bank(a):
            return misc[0] if a.turn is None and a.base == 0 else misc[1]

        W_ORDER = (1, 0, 2, 3)
        block = stack.enter_context(nc.Block())

        @block.sync
        def _(sp):
            def load(at):
                if at.turn is not None or at.base >= 2:
                    sp.wait_ge(xn_done, at.back(2).count(1, 1))
                    sp.wait_ge(c_tp_ready, at.back(2).count(1, 1))
                b = bass.ds(at.n(), 1)
                sp.dma_start(c_in[:, at.u, :, :],
                             ctx_in[b, :, :].rearrange("b (t p) d -> p (b t) d", p=P)).then_inc(c_loaded[at.u], 16)
                sp.dma_start(x_in[:, b, :, :].rearrange("p b t d -> p (b t) d"),
                             x[b, :, :].rearrange("b (t p) d -> p (b t) d", p=P)).then_inc(x_loaded[at.u], 16)

            def stack_parts(at, c):
                first = at.turn is None and at.base < 2
                heads = slice(c * HC, (c + 1) * HC)
                if c == 1:
                    if not first:
                        sp.wait_ge(st_ready, at.back(2).count(16, 16))
                elif first:
                    sp.wait_ge(k_lo_done, at.count(2, 2))
                else:
                    sp.wait_ge(q_lo_done, at.count(2, 2))
                for i, k_part in enumerate((k_hi, k_hi, k_lo, k_lo)):
                    sp.dma_start(k_st[at.u][i * DK:(i + 1) * DK, heads, :].bitcast(FP32),
                                 k_part[:, at.u, c, :].bitcast(FP32)).then_inc(stacked[at.u][c], 16)
                if c == 0 and first:
                    sp.wait_ge(q_lo_done, at.count(2, 2))
                    sp.wait_ge((q0_zeroed, q1_zeroed)[at.u], 1)
                for i, q_part in enumerate((q_hi, q_lo, q_hi, q_lo)):
                    sp.dma_start(q_st[at.u][i * DK:(i + 1) * DK, heads, :].bitcast(FP32),
                                 q_part[:, at.u, c, :].bitcast(FP32)).then_inc(stacked[at.u][c], 16)
                sp.dma_start(q_st[at.u][PARTS:PARTS + 2, heads, :].bitcast(FP32),
                             k_st[0][PARTS + 2:PARTS + 4, 0:HC, :].bitcast(FP32)).then_inc(stacked[at.u][c], 16)

            def store_max(at, c):
                sp.wait_ge(max_t_copied, at.count(2, c + 1))
                sp.dma_start(q_st[at.u][PARTS:PARTS + 2, c * HC:(c + 1) * HC, :].bitcast(FP32),
                             max_t[c][:, :].bitcast(FP32)).then_inc(max_stored[at.u][c], 16)

            load(At(0))
            for i, bias in enumerate((bq, bk)):
                for c in range(C):
                    sp.dma_start(bqk[:, i, c:c + 1], bias[c * P:(c + 1) * P].rearrange("(h r a) -> r h a", r=DK, a=1),
                                  allow_slow_non_contiguous=True).then_inc(bias_in, 16)
            sp.dma_start(bv_bc[:, :], bv.partition_broadcast(P)).then_inc(bias_in, 16)
            for w, i in ((wv, 2), (wo, 3)):
                sp.dma_start(w_raw[:, i, :, :], w.rearrange("(c p) i -> p c i", p=P)).then_inc(weight_in[i], 16)
            load(At(1))
            sp.wait_ge(ones_done, 1)
            for u, zeroed in enumerate((k0_zeroed, k1_zeroed)):
                sp.wait_ge(zeroed, 1)
                sp.dma_start(k_st[u][PARTS:PARTS + 2, :, :].bitcast(FP32), ones[0:2 * H * S // P, :]).then_inc(ones_stored, 16)
            sp.wait_ge(ones_stored, 16 * 2)

            def load_params():
                sp.dma_start(w1_sb[:, :, :], w1.rearrange("(c p) i -> p c i", p=P)).then_inc(params_in, 16)
                sp.dma_start(w2_sb[:, :, :], w2.rearrange("(c p) i -> p c i", p=P)).then_inc(params_in, 16)
                sp.dma_start(w3_sb[:, :], w3).then_inc(params_in, 16)
                sp.dma_start(gw1_sb[:, :, :], gw1.rearrange("(c p) i -> p c i", p=P)).then_inc(params_in, 16)
                sp.dma_start(gw2_sb[:, :], gw2).then_inc(params_in, 16)

            def step(st):
                a, b, c = st.batch("A"), st.batch("B"), st.batch("C")
                if c:
                    store_max(c, 1)
                if a:
                    stack_parts(a, 0)
                if b:
                    store_max(b, 0)
                if st.turn is not None or st.base + 2 < B:
                    load(At(st.base + 2, st.turn))
                if a:
                    stack_parts(a, 1)
                if st.turn is None and st.base == 1:
                    load_params()

            run_steps(sp, step, LOAD_LOOP)

            with sp.Fori(0, B // 2) as turn:
                for u in range(2):
                    at = At(u, turn)
                    sp.wait_ge(fin_done, at.count(1, 1))
                    b = bass.ds(at.n(), 1)
                    sp.dma_start(out[b, :, :].rearrange("b (t p) d -> p (b t) d", p=P),
                                 fin[u]).then_inc(stored_u[u], 16)
            for u in range(2):
                sp.wait_ge(stored_u[u], 16 * (B // 2))

        @block.gpsimd
        def _(pool):
            nc.gpsimd.memset(ident[:, :], 0.0).then_inc(ident_done, 1)
            pool.wait_ge(ident_done, 1)
            nc.gpsimd.affine_select(out=ident[:, :], in_=ident[:, :], compare_op=ALU.not_equal, fill=1.0,
                                    base=0, pattern=[[-1, P]], channel_multiplier=1).then_inc(ident_done, 1)
            nc.gpsimd.memset(half_neg[:, :], -0.5).then_inc(half_neg_done, 1)
            nc.gpsimd.memset(eps[:, :], EPS).then_inc(half_neg_done, 1)
            pool.wait_ge(half_neg_done, 2)
            nc.gpsimd.memset(k_st[0][64:P, :, :].bitcast(FP32), 0.0).then_inc(k0_zeroed, 1)
            pool.wait_ge(k0_zeroed, 1)

            def load_small(pairs, done):
                for dst, src in pairs:
                    pool.dma_start(dst, src, allow_slow_non_contiguous=True).then_inc(done, 16)

            def zero_rest():
                pool.wait_ge(rstd_done, 1)
                nc.gpsimd.memset(q_st[0][64:P, :, :].bitcast(FP32), 0.0).then_inc(q0_zeroed, 1)
                pool.wait_ge(q0_zeroed, 1)
                nc.gpsimd.memset(w4_col[:, :], 0.0).then_inc(w4_zeroed, 1)
                pool.wait_ge(w4_zeroed, 1)
                nc.gpsimd.memset(q_st[1][64:P, :, :].bitcast(FP32), 0.0).then_inc(q1_zeroed, 1)
                pool.wait_ge(q1_zeroed, 1)

            def load_gates():
                load_small(((bo_bc[:, :], bo.partition_broadcast(P)),
                            (scal[:, 0:1], g_xattn.partition_broadcast(P)),
                            (scal[:, 1:2], g_ffn.partition_broadcast(P)),
                            (scal[:, 2:3], arange.partition_broadcast(P)),
                            (scal[:, 3:4], b4.partition_broadcast(P)),
                            (scal[:, 4:5], gb3.partition_broadcast(P))), gates_in)

            def load_ffn():
                load_small(((b1_sb[:, 0:1], b1[0:P].rearrange("(p a) -> p a", a=1)),
                            (b1_sb[:, 1:2], b1[P:D].rearrange("(p a) -> p a", a=1)),
                            (b2_sb[:, :], b2.rearrange("(p a) -> p a", a=1)),
                            (b3_sb[0:64, :], b3.rearrange("(p a) -> p a", a=1)),
                            (b3_sb[64:P, :], b3.rearrange("(p a) -> p a", a=1)),
                            (gb1_sb[:, :], gb1.rearrange("(p a) -> p a", a=1)),
                            (gb2_sb[:, :], gb2.rearrange("(p a) -> p a", a=1)),
                            (gw3_col[:, :], gw3),
                            (w4_col[0:64, 0:1], w4),
                            (w4_col[64:P, 1:2], w4)), small_in)

            def step(st):
                a, d = st.batch("A"), st.batch("D")
                if a:
                    pool.wait_ge(aggr_done, a.count(2, 2))
                    nc.gpsimd.tensor_tensor(var_eps[:, :], mean_var[:, :, 1], eps[:, :], ALU.add).then_inc(rstd_added, 1)
                    pool.wait_ge(rstd_added, a.count(1, 1))
                    if a.turn is not None or a.base >= 1:
                        pool.wait_ge(xn_done, a.count(1, 0))
                    nc.gpsimd.tensor_tensor(rstd[:, :], var_eps[:, :], half_neg[:, :], ALU.pow).then_inc(rstd_done, 1)
                if d:
                    pool.wait_ge(gates_ready, 1)
                    if d.turn is not None or d.base >= 1:
                        pool.wait_ge(x2_done, d.count(1, 0))
                    b = bass.ds(d.n(), 1)
                    for t in range(TC):
                        ins = nc.gpsimd.tensor_tensor(x_b[:, t, :], x_in[:, b, t, :].rearrange("p b d -> p (b d)"),
                                                      thbo[:, :], ALU.add)
                        ins.then_inc(xb_done, 1)
                    pool.wait_ge(aggr2_done, d.count(2, 2))
                    nc.gpsimd.tensor_tensor(var_eps2[:, :], mean_var2[:, :, 1], eps[:, :], ALU.add).then_inc(rstd2_added, 1)
                    pool.wait_ge(rstd2_added, d.count(1, 1))
                    nc.gpsimd.tensor_tensor(rstd2[:, :], var_eps2[:, :], half_neg[:, :], ALU.pow).then_inc(rstd2_done, 1)
                if st.turn is None and st.base < 3:
                    (zero_rest, load_gates, load_ffn)[st.base]()

            run_steps(pool, step)

        @block.tensor
        def _(pe):
            pe.wait_ge(ident_done, 2)

            def transpose_weight(i, psum):
                w = W_ORDER[i]
                pe.wait_ge(weight_in[w], 16)
                for ci in range(C):
                    for co in range(C):
                        last = nc.tensor.transpose(psum[:, ci * D + co * P:ci * D + (co + 1) * P],
                                                   w_raw[:, w, co, ci * P:(ci + 1) * P], ident[:, :])
                last.then_inc(w_tp_ready, 1)

            for i in range(2):
                transpose_weight(i, misc[i])

            def transposes(psum, src, ready):
                for c in range(C):
                    for t in range(TC):
                        last = nc.tensor.transpose(psum[:, c * S + t * P:c * S + (t + 1) * P],
                                                   src[:, t, c * P:(c + 1) * P], ident[:, :])
                last.then_inc(ready, 1)

            def project(psum, w, src, ready):
                for co in range(C):
                    for ci in range(C):
                        last = nc.tensor.matmul(psum[:, co * S:(co + 1) * S], w_t[:, w, ci, co * P:(co + 1) * P],
                                                src[:, ci, :], start=(ci == 0), stop=(ci == C - 1))
                last.then_inc(ready, 1)

            def scores_max_pass(b, j):
                if j % 4 == 0:
                    c = j // 4
                    pe.wait_ge(stacked[b.u][c], b.count_of_parity(16 * 9))
                for t in range(TC):
                    n = 2 * j + t
                    if b.turn is not None or b.base > 0 or n >= 2:
                        pe.wait_ge(s1_maxed, b.count(16, n - 1))
                    for i in range(2):
                        h = 2 * j + i
                        last = nc.tensor.matmul(s1_bank[t][:, i * S:(i + 1) * S],
                                                q_st[b.u][:, h, t * P:(t + 1) * P], k_st[b.u][:, h, :],
                                                start=True, stop=True)
                    last.then_inc(s1_ready, 1)

            def scores_exp_pass(c, j):
                g, t = j // 2, j % 2
                if j % 4 == 0:
                    pe.wait_ge(max_stored[c.u][j // 4], c.count_of_parity(16))
                for i in range(2):
                    n = 2 * j + i
                    if c.turn is not None or c.base > 0 or n >= 2:
                        pe.wait_ge(exp_done, c.count(16, n - 1))
                    for e in range(2):
                        h = 4 * g + 2 * i + e
                        last = nc.tensor.matmul(st_bank[i][:, e * S:(e + 1) * S],
                                                k_st[c.u][:, h, t * P:(t + 1) * P], q_st[c.u][:, h, :],
                                                start=True, stop=True)
                    last.then_inc(st_ready, 1)

            def times_values(c, j):
                g, t = j // 2, j % 2
                pe.wait_ge(exp_done, c.count(16, 2 * j + 2))
                if j == 0:
                    pe.wait_ge(v_done, c.count(1, 1))
                if t == 0 and (c.turn is not None or c.base > 0 or g >= 2):
                    pe.wait_ge(o_t_copied, c.count(4, g - 1))
                for i in range(4):
                    last = nc.tensor.matmul(pv_bank[g % 2][SLOT * i:SLOT * (i + 1), 0:S],
                                            v_sl[:, c.u, t, 4 * g + i, :], probs[:, j % 2, i, :],
                                            start=(t == 0), stop=(t == TC - 1))
                last.then_inc(pv_done, 1)

            def transpose_max(st, at, c):
                pe.wait_ge(max_parts_done, at.count(2, c + 1))
                psum = free_bank(pe, st, f"max{c}")
                nc.tensor.transpose(psum[0:2 * HC * TC, 0:P],
                                    max_parts[:, c, :, :, :].bitcast(FP32).rearrange("p a h t -> p (a h t)"),
                                    ident[:, :]).then_inc(max_tp_ready, 1)

            def transpose_outputs(st, d, half):
                pe.wait_ge(o_t_copied, d.count(4, 2 * half + 2))
                psum = free_bank(pe, st, "o_a" if half == 0 else "o_b")
                for t in range(TC):
                    for i in range(2):
                        last = nc.tensor.transpose(psum[:, (2 * t + i) * P:(2 * t + i + 1) * P],
                                                   o_t[:, d.u, 2 * half + i, t * P:(t + 1) * P], ident[:, :])
                last.then_inc(o_tp_ready, 1)

            def first_projections(a):
                pe.wait_ge(c_loaded[0], 16)
                pe.wait_ge(w_t_copied, 2)
                transposes(misc[1], c_in[:, 0, :, :], c_tp_ready)
                pe.wait_ge(xn_done, 1)
                transposes(query_bank(a), xn, x_tp_ready)
                pe.wait_ge(c_t_copied, 1)
                project(misc[1], 1, c_t[:, 0, :, :], k_ready)
                pe.wait_ge(x_t_copied, 1)
                project(query_bank(a), 0, x_t, q_ready)
                pe.wait_ge(q_lo_done, 2)
                for i in range(2, 4):
                    transpose_weight(i, misc[0])
                    pe.wait_ge(w_t_copied, i + 1)

            def step(st):
                a, b, c, d = (st.batch(x) for x in STAGES)
                if st.turn is None and st.base == 0:
                    first_projections(a)
                    return
                for j in range(8):
                    if c:
                        scores_exp_pass(c, j)
                    if j == 0 and d:
                        times_values(d, 7)
                    if j > 0 and c:
                        times_values(c, j - 1)
                    if j == 0 and a:
                        pe.wait_ge(c_loaded[a.u], a.count_of_parity(16))
                        transposes(free_bank(pe, st, "c_t"), c_in[:, a.u, :, :], c_tp_ready)
                    if b:
                        scores_max_pass(b, j)
                    if j == 0 and c:
                        transpose_max(st, c, 1)
                    if j == 1:
                        if d:
                            transpose_outputs(st, d, 0)
                        if a:
                            pe.wait_ge(c_t_copied, a.count(1, 1))
                            project(free_bank(pe, st, "k"), 1, c_t[:, a.u, :, :], k_ready)
                    if j == 2:
                        if d:
                            transpose_outputs(st, d, 1)
                        if a:
                            pe.wait_ge(xn_done, a.count(1, 1))
                            transposes(free_bank(pe, st, "x_t"), xn, x_tp_ready)
                    if j == 3:
                        if a:
                            pe.wait_ge(x_t_copied, a.count(1, 1))
                            project(free_bank(pe, st, "q"), 0, x_t, q_ready)
                        if d:
                            pe.wait_ge(o_normed, d.count(2, 2))
                            transposes(free_bank(pe, st, "o_nt"), o_n, o_nt_ready)
                    if j == 4 and d:
                        pe.wait_ge(o_nt_copied, d.count(1, 1))
                        psum = free_bank(pe, st, "y")
                        for t in range(TC):
                            for ci in range(C):
                                last = nc.tensor.matmul(psum[:, t * D:(t + 1) * D], o_nt[:, ci, t * P:(t + 1) * P],
                                                        w_t[:, 3, ci, :], start=(ci == 0), stop=(ci == C - 1))
                        last.then_inc(y_ready, 1)
                    if j == 5 and b:
                        transpose_max(st, b, 0)
                    if j == 6 and b:
                        pe.wait_ge(c_t_copied, b.count(1, 1))
                        psum = free_bank(pe, st, "v")
                        for t in range(TC):
                            for ci in range(C):
                                last = nc.tensor.matmul(psum[:, t * D:(t + 1) * D], c_t[:, b.u, ci, t * P:(t + 1) * P],
                                                        w_t[:, 2, ci, :], start=(ci == 0), stop=(ci == C - 1))
                        last.then_inc(v_ready, 1)
                    if j == 7 and d:
                        pe.wait_ge(x2n_done, d.count(1, 1))
                        transposes(free_bank(pe, st, "x2_t"), x2n, x2_tp_ready)

            run_steps(pe, step)

            def layer1(n, co):
                p = n % PAIRS
                if n >= PAIRS:
                    pe.wait_ge(moved_done, 2 * (n - PAIRS) + 2)
                if n >= 2:
                    pe.wait_ge(g1_done, 2 * (n - 2) + co + 1)
                for ci in range(C):
                    last = nc.tensor.matmul(l1_bank[n % 2][co][:, :], w1_sb[:, ci, co * P:(co + 1) * P],
                                            state[:, ci, 2 * p:2 * p + 2, :].rearrange("p b s -> p (b s)"),
                                            start=(ci == 0), stop=(ci == C - 1))
                last.then_inc(l1_ready, 1)

            def layer2(n):
                pe.wait_ge(g1_done, 2 * n + 2)
                if n >= 1:
                    pe.wait_ge(g2_done, n)
                for ci in range(C):
                    last = nc.tensor.matmul(l2_bank[:, :], w2_sb[:, ci, :], h1[n % 2][:, ci, :],
                                            start=(ci == 0), stop=(ci == C - 1))
                last.then_inc(l2_ready, 1)

            def layer3(n):
                pe.wait_ge(g2_done, n + 1)
                if n >= 1:
                    pe.wait_ge(g3_done, n)
                for half in range(2):
                    last = nc.tensor.matmul(l3_bank[64 * half:64 * (half + 1), 0:S], w3_sb[:, :],
                                            h2[n % 2][:, half * S:(half + 1) * S], start=True, stop=True)
                last.then_inc(l3_ready, 1)

            def layer4(n):
                pe.wait_ge(g3_done, n + 1)
                if n >= 1:
                    pe.wait_ge(tanh_z_done, n)
                for half in range(2):
                    last = nc.tensor.matmul(l4_bank[:, half * S:(half + 1) * S], w4_rep[:, half, :], h3[n % 2],
                                            start=True, stop=True)
                last.then_inc(l4_ready, 1)

            def ffn_step(n):
                if n < CYCLES * PAIRS:
                    layer1(n, 0)
                if 0 <= n - 2:
                    layer3(n - 2)
                if n < CYCLES * PAIRS:
                    layer1(n, 1)
                if 0 <= n - 2:
                    layer4(n - 2)
                if 0 <= n - 1 < CYCLES * PAIRS:
                    layer2(n - 1)

            pe.wait_ge(state_ready, 2 * B)
            ffn_step(0)
            pe.wait_ge(params_in, 16 * 5)
            for ci in range(C):
                last = nc.tensor.matmul(l4_bank[:, 0:B], gw1_sb[:, ci, :], sums[:, ci, :],
                                        start=(ci == 0), stop=(ci == C - 1))
            last.then_inc(gl_ready, 1)
            pe.wait_ge(gl_done, 1)
            nc.tensor.matmul(l4_bank[0:64, 64:64 + B], gw2_sb[:, :], gh1[:, :], start=True, stop=True).then_inc(gl_ready, 1)
            ffn_step(1)
            pe.wait_ge(gl_done, 2)
            nc.tensor.matmul(l4_bank[:, 128:128 + B], gw3_rep[:, :], gh2[:, :], start=True, stop=True).then_inc(gl_ready, 1)
            pe.wait_ge(gl_done, 3)
            for n in range(2, CYCLES * PAIRS + 2):
                ffn_step(n)

            for b in range(B):
                pe.wait_ge(moved_done, 2 * ((CYCLES - 1) * PAIRS + b // 2) + 2)
                if b >= 2:
                    pe.wait_ge(fin_done, b - 1)
                else:
                    pe.wait_ge(g1_done, 2 * CYCLES * PAIRS)
                for t in range(TC):
                    for ci in range(C):
                        last = nc.tensor.transpose(l1_bank[b % 2][0][:, t * D + ci * P:t * D + (ci + 1) * P],
                                                   state[:, ci, b, t * P:(t + 1) * P], ident[:, :])
                last.then_inc(fin_tp_ready, 1)

        @block.scalar
        def _(act):
            for i, w in ((1, wk), (0, wq)):
                act.dma_start(w_raw[:, i, :, :], w.rearrange("(c p) i -> p c i", p=P)).then_inc(weight_in[i], 16)

            def copy_weight(i, psum):
                w = W_ORDER[i]
                act.wait_ge(w_tp_ready, i + 1)
                src = psum[:, :].rearrange("p (a n) -> p a n", a=2 * C)
                dst = w_t[:, w, :, :].rearrange("p a (c n) -> p (a c) n", c=C)
                if w < 2:
                    src = src.rearrange("p a (h r) -> p a h r", r=DK)
                    dst = dst.rearrange("p a (r h) -> p a h r", r=DK)
                nc.scalar.copy(dst, src).then_inc(w_t_copied, 1)

            for i in range(2):
                copy_weight(i, misc[i])

            def project_hi(at, i, dst, ready, done, psum):
                if at.turn is None and at.base == 0 and i == 1:
                    act.wait_ge(bias_in, 16 * 5)
                act.wait_ge(ready, at.count(1, 1))
                for c in range(C):
                    nc.scalar.activation(dst[:, at.u, c, :], psum[:, c * S:(c + 1) * S], ACT.Identity,
                                         bias=bqk[:, i, c:c + 1]).then_inc(done, 1)

            def copy_x_t(a):
                act.wait_ge(x_tp_ready, a.count(1, 1))
                nc.scalar.copy(x_t[:, :, :].rearrange("p c s -> p (c s)"), query_bank(a)[:, :]).then_inc(x_t_copied, 1)

            def copy_max(at, c, m):
                act.wait_ge(max_tp_ready, at.count(2, c + 1))
                if at.turn is not None or at.base >= 1:
                    last = at.back(1)
                    act.wait_ge(max_stored[last.u][c], last.count_of_parity(16))
                nc.scalar.copy(max_t[c][:, :], misc[m][0:2 * HC * TC, 0:P]).then_inc(max_t_copied, 1)

            def copy_outputs(at, g):
                act.wait_ge(pv_done, at.count(8, 2 * g + 2))
                nc.scalar.copy(o_t[:, at.u, g, :], pv_bank[g % 2][:, 0:S]).then_inc(o_t_copied, 1)

            def step(st):
                a, b, c, d = (st.batch(x) for x in STAGES)
                for j in range(8):
                    if c:
                        for i in range(2):
                            act.wait_ge(st_ready, c.count(16, 2 * j + i + 1))
                            if i == 0 and (c.turn is not None or c.base > 0 or j >= 2):
                                act.wait_ge(pv_done, c.count(8, j - 1))
                            nc.scalar.activation(probs[:, j % 2, 2 * i:2 * i + 2, :].rearrange("p e s -> p (e s)"),
                                                 st_bank[i][:, :], ACT.Exp, scale=DK ** -0.5).then_inc(exp_done, 1)
                    if j == 0 and d:
                        copy_outputs(d, 3)
                    if j == 0 and a:
                        act.wait_ge(c_tp_ready, a.count(1, 1))
                        nc.scalar.copy(c_t[:, a.u, :, :].rearrange("p c s -> p (c s)"), misc[1][:, :]).then_inc(c_t_copied, 1)
                    if j == 0 and c:
                        copy_max(c, 1, 0)
                    if j == 1 and a:
                        if st.turn is None and st.base == 0:
                            copy_x_t(a)
                        project_hi(a, 1, k_hi, k_ready, k_hi_done, misc[1])
                    if j == 2 and a and (st.turn is not None or st.base > 0):
                        copy_x_t(a)
                    if j == 2 and c:
                        copy_outputs(c, 0)
                    if j == 3 and a:
                        project_hi(a, 0, q_hi, q_ready, q_hi_done, query_bank(a))
                    if j == 3 and d:
                        act.wait_ge(o_nt_ready, d.count(1, 1))
                        nc.scalar.copy(o_nt[:, :, :].rearrange("p c s -> p (c s)"), misc[0][:, :]).then_inc(o_nt_copied, 1)
                    if j == 4 and c:
                        copy_outputs(c, 1)
                    if j == 5 and b:
                        copy_max(b, 0, 1)
                    if j == 6 and c:
                        copy_outputs(c, 2)
                    if j == 7 and d:
                        act.wait_ge(x2_tp_ready, d.count(1, 1))
                        for ci in range(C):
                            nc.scalar.activation(state[:, ci, bass.ds(d.n(), 1), :].rearrange("p b s -> p (b s)"),
                                                 misc[0][:, ci * S:(ci + 1) * S], ACT.Identity,
                                                 accum_out=sums[:, ci, bass.ds(d.n(), 1)]).then_inc(state_ready, 1)
                if st.turn is None and st.base == 0:
                    for i in range(2, 4):
                        copy_weight(i, misc[0])
                if st.turn is None and st.base == 2:
                    act.wait_ge(gates_in, 16 * 6)
                    nc.scalar.activation(tanh_g[:, :], scal[:, 0:2], ACT.Tanh).then_inc(tanh_done, 1)

            run_steps(act, step)

            def gelu1(n):
                for co in range(C):
                    act.wait_ge(l1_ready, 2 * n + co + 1)
                    if co == 0 and n >= 2:
                        act.wait_ge(l2_ready, n - 1)
                    nc.scalar.activation(h1[n % 2][:, co, :], l1_bank[n % 2][co][:, :], ACT.Gelu,
                                         bias=b1_sb[:, co:co + 1]).then_inc(g1_done, 1)

            def gelu2(n):
                act.wait_ge(l2_ready, n + 1)
                if n >= 2:
                    act.wait_ge(l3_ready, n - 1)
                nc.scalar.activation(h2[n % 2], l2_bank[:, :], ACT.Gelu, bias=b2_sb[:, :]).then_inc(g2_done, 1)

            def gelu3(n):
                act.wait_ge(l3_ready, n + 1)
                if n >= 2:
                    act.wait_ge(l4_ready, n - 1)
                nc.scalar.activation(h3[n % 2], l3_bank[:, 0:S], ACT.Gelu, bias=b3_sb[:, :]).then_inc(g3_done, 1)

            def tanh_z(n):
                act.wait_ge(l4_ready, n + 1)
                if n >= 2:
                    act.wait_ge(coup_done, 2 * (n - 1))
                nc.scalar.activation(tz[n % 2], l4_bank[:, :], ACT.Tanh, bias=half_b[:, 0:1], scale=0.5).then_inc(tanh_z_done, 1)

            act.wait_ge(prep_done, 1)
            act.wait_ge(gl_ready, 1)
            nc.scalar.activation(gh1[:, :], l4_bank[:, 0:B], ACT.Gelu, bias=gb1_sb[:, :], scale=1.0 / S).then_inc(gl_done, 1)
            gelu1(0)
            act.wait_ge(gl_ready, 2)
            nc.scalar.activation(gh2[:, :], l4_bank[0:64, 64:64 + B], ACT.Gelu, bias=gb2_sb[:, :]).then_inc(gl_done, 1)
            gelu1(1)
            gelu2(0)
            act.wait_ge(gl_ready, 3)
            nc.scalar.activation(gz[:, :], l4_bank[:, 128:128 + B], ACT.Tanh, bias=half_b[:, 1:2], scale=0.5).then_inc(gl_done, 1)
            for n in range(2, CYCLES * PAIRS + 2):
                gelu3(n - 2)
                if n < CYCLES * PAIRS:
                    gelu1(n)
                tanh_z(n - 2)
                if n - 1 < CYCLES * PAIRS:
                    gelu2(n - 1)

        @block.vector
        def _(dve):
            nc.vector.memset(ones[:, :], 1.0).then_inc(ones_done, 1)
            nc.vector.memset(k_st[1][64:P, :, :].bitcast(FP32), 0.0).then_inc(k1_zeroed, 1)

            def prepare_values():
                nc.vector.memset(v_sl[:, :, :, :, DK:SLOT].rearrange("p u t h e -> p (u t h) e"), 0.0).then_inc(v_zeroed, 1)
                dve.wait_ge(v_zeroed, 1)
                nc.vector.memset(v_sl[:, :, :, :, DK:DK + 1].rearrange("p u t h e -> p (u t h) e"), 1.0).then_inc(v_ones, 1)

            def prepare_gates():
                dve.wait_ge(tanh_done, 1)
                nc.vector.tensor_scalar(thbo[:, :], bo_bc[:, :], tanh_g[:, 0:1], None, ALU.mult).then_inc(gates_ready, 1)

            def prepare_ffn():
                dve.wait_ge(small_in, 16 * 10)
                for half in range(2):
                    nc.vector.tensor_scalar(w4_rep[:, half, :], ones[:, :], w4_col[:, half:half + 1], None, ALU.mult)
                nc.vector.tensor_scalar(gw3_rep[:, :], ones[0:64, :], gw3_col[:, :], None, ALU.mult)
                nc.vector.tensor_scalar(half_b[:, :], scal[:, 3:5], 0.5, None, ALU.mult)
                nc.vector.tensor_scalar(gain[:, 0:1], scal[:, 2:3], 0.3, None, ALU.mult)
                nc.vector.tensor_scalar(gain[:, 1:2], scal[:, 2:3], 0.7, None, ALU.mult)
                nc.vector.memset(sign[0:64, :], 1.0)
                nc.vector.memset(sign[64:P, :], -1.0).then_inc(prep_done, 1)

            def max_of(b, j):
                for t in range(TC):
                    dve.wait_ge(s1_ready, b.count(16, 2 * j + t + 1))
                    nc.vector.tensor_reduce(neg_max[:, j // 4, 2 * (j % 4):2 * (j % 4) + 2, t],
                                            s1_bank[t][:, :].rearrange("p (e s) -> p e s", e=2),
                                            AX.X, ALU.max, negate=True).then_inc(s1_maxed, 1)

            def split_max(at, c):
                dve.wait_ge(s1_maxed, at.count(16, 8 * (c + 1)))
                if at.turn is not None or at.base >= 1:
                    dve.wait_ge(max_tp_ready, at.count(2, c - 1))
                nm = neg_max[:, c, :, :].rearrange("p h t -> p (h t)")
                hi, lo = (max_parts[:, c, i, :, :].rearrange("p h t -> p (h t)") for i in range(2))
                nc.vector.tensor_copy(hi, nm).then_inc(max_hi_done, 1)
                dve.wait_ge(max_hi_done, at.count(2, c + 1))
                nc.vector.tensor_tensor(lo, nm, hi.bitcast(FP32), ALU.subtract).then_inc(max_parts_done, 1)

            def project_lo(at, i, hi, lo, hi_done, done, psum):
                dve.wait_ge(hi_done, at.count(2, 2))
                for c in range(C):
                    nc.vector.scalar_tensor_tensor(lo[:, at.u, c, :], psum[:, c * S:(c + 1) * S], bqk[:, i, c:c + 1],
                                                   hi[:, at.u, c, :].bitcast(FP32), ALU.add, ALU.subtract).then_inc(done, 1)

            def norm_outputs(d, half):
                dve.wait_ge(o_tp_ready, d.count(2, half + 1))
                src = misc[0][:, :].rearrange("p (t h e) -> p t h e", t=TC, e=SLOT)
                rd = rden[:, :, :, :].rearrange("p t g i -> p t (g i)")
                nc.vector.reciprocal(rd, src[:, :, :, DK]).then_inc(rden_done, 1)
                dve.wait_ge(rden_done, d.count(2, half + 1))
                if half == 0 and (d.turn is not None or d.base >= 1):
                    dve.wait_ge(o_nt_ready, d.count(1, 0))
                nc.vector.tensor_tensor(o_n[:, :, half * P:(half + 1) * P].rearrange("p t (h e) -> p t h e", e=DK),
                                        src[:, :, :, 0:DK], rd.unsqueeze(3).to_broadcast([P, TC, HC, DK]),
                                        ALU.mult).then_inc(o_normed, 1)

            def statistics(src, out_stats, out_mean_var, done):
                for t in range(TC):
                    nc.vector.bn_stats(out_stats[:, t, :], src(t))
                dve.drain()
                for t in range(TC):
                    nc.vector.bn_aggr(out_mean_var[:, t, :], out_stats[:, t, :]).then_inc(done, 1)

            def step(st):
                a, b, c, d = (st.batch(x) for x in STAGES)
                x_of = lambda t: x_in[:, bass.ds(a.n(), 1), t, :].rearrange("p b d -> p (b d)")
                x2_of = lambda t: x2[:, bass.ds(d.n(), 1), t, :].rearrange("p b d -> p (b d)")
                for j in range(8):
                    if j == 0:
                        if c:
                            split_max(c, 1)
                        if a:
                            dve.wait_ge(x_loaded[a.u], a.count_of_parity(16))
                            statistics(x_of, stats, mean_var, aggr_done)
                    if j == 1 and a:
                        dve.wait_ge(rstd_done, a.count(1, 1))
                        if a.turn is not None or a.base >= 1:
                            dve.wait_ge(x_tp_ready, a.count(1, 0))
                        for t in range(TC):
                            last = nc.vector.tensor_scalar(xn[:, t, :], x_of(t), mean_var[:, t, 0:1], rstd[:, t:t + 1],
                                                           ALU.subtract, ALU.mult)
                        last.then_inc(xn_done, 1)
                    if j == 2 and a:
                        project_lo(a, 1, k_hi, k_lo, k_hi_done, k_lo_done, misc[1])
                    if j == 4:
                        if a:
                            project_lo(a, 0, q_hi, q_lo, q_hi_done, q_lo_done, query_bank(a))
                        if b:
                            split_max(b, 0)
                    if j == 5 and d:
                        dve.wait_ge(y_ready, d.count(1, 1))
                        dve.wait_ge(xb_done, d.count(2, 2))
                        nc.vector.scalar_tensor_tensor(x2[:, bass.ds(d.n(), 1), :, :].rearrange("p b t d -> p (b t d)"),
                                                       misc[0][:, :], tanh_g[:, 0:1], x_b[:, :, :].rearrange("p t d -> p (t d)"),
                                                       ALU.mult, ALU.add).then_inc(x2_done, 1)
                        dve.drain()
                        statistics(x2_of, stats2, mean_var2, aggr2_done)
                    if j == 6 and d:
                        dve.wait_ge(rstd2_done, d.count(1, 1))
                        for t in range(TC):
                            last = nc.vector.tensor_scalar(x2n[:, t, :], x2_of(t), mean_var2[:, t, 0:1], rstd2[:, t:t + 1],
                                                           ALU.subtract, ALU.mult)
                        last.then_inc(x2n_done, 1)
                    if b:
                        max_of(b, j)
                    if j == 1 and d:
                        norm_outputs(d, 0)
                    if j == 2 and d:
                        norm_outputs(d, 1)
                    if j == 6 and b:
                        dve.wait_ge(v_ready, b.count(1, 1))
                        if b.turn is None and b.base == 0:
                            dve.wait_ge(v_ones, 1)
                        nc.vector.tensor_tensor(v_sl[:, b.u, :, :, 0:DK], misc[1][:, :].rearrange("p (t h e) -> p t h e", t=TC, e=DK),
                                                bv_bc[:, :].rearrange("p (h e) -> p h e", e=DK).unsqueeze(1).to_broadcast([P, TC, H, DK]),
                                                ALU.add).then_inc(v_done, 1)
                if st.turn is None:
                    if st.base == 0:
                        prepare_values()
                    if st.base == 2:
                        prepare_gates()
                    if st.base == 3:
                        prepare_ffn()

            run_steps(dve, step)

            dve.wait_ge(gl_done, 3)
            nc.vector.tensor_scalar(base_c[:, :], gz[:, :], gain[:, 1:2], 0.1, ALU.mult, ALU.add).then_inc(base_done, 1)
            dve.wait_ge(base_done, 1)
            for n in range(CYCLES * PAIRS):
                p = n % PAIRS
                dve.wait_ge(tanh_z_done, n + 1)
                for half in range(2):
                    nc.vector.tensor_scalar(coup[n % 2][:, half * S:(half + 1) * S], tz[n % 2][:, half * S:(half + 1) * S],
                                            gain[:, 0:1], base_c[:, 2 * p + half:2 * p + half + 1],
                                            ALU.mult, ALU.add).then_inc(coup_done, 1)
                dve.wait_ge(coup_done, 2 * n + 2)
                half_state = [state[:, ci, 2 * p:2 * p + 2, :].rearrange("p b s -> p (b s)") for ci in range(C)]
                for ci in range(C):
                    nc.vector.scalar_tensor_tensor(twist[n % 2][:, ci, :], half_state[1 - ci], sign[:, :], coup[n % 2],
                                                   ALU.mult, ALU.mult).then_inc(twist_done, 1)
                for ci in range(C):
                    dve.wait_ge(twist_done, 2 * n + 2)
                    nc.vector.tensor_tensor(half_state[ci], half_state[ci], twist[n % 2][:, ci, :],
                                            ALU.add if ci == 0 else ALU.subtract).then_inc(moved_done, 1)
            for b in range(B):
                dve.wait_ge(fin_tp_ready, b + 1)
                if b >= 2:
                    dve.wait_ge(stored_u[b % 2], 16 * (b // 2))
                nc.vector.scalar_tensor_tensor(fin[b % 2].rearrange("p t d -> p (t d)"), l1_bank[b % 2][0][:, :], tanh_g[:, 1:2],
                                               x2[:, b, :, :].rearrange("p t d -> p (t d)"), ALU.mult, ALU.add).then_inc(fin_done, 1)


_INS = ['x', 'ctx_1024', 'g_xattn', 'g_ffn', 'L0_xattn_Wq', 'L0_xattn_bq', 'L0_xattn_Wk', 'L0_xattn_bk',
        'L0_xattn_Wv', 'L0_xattn_bv', 'L0_xattn_Wo', 'L0_xattn_bo',
        'L0_ffn_cn_w1', 'L0_ffn_cn_b1', 'L0_ffn_cn_w2', 'L0_ffn_cn_b2', 'L0_ffn_cn_w3', 'L0_ffn_cn_b3',
        'L0_ffn_cn_w4', 'L0_ffn_cn_b4', 'L0_ffn_gc_w1', 'L0_ffn_gc_b1', 'L0_ffn_gc_w2', 'L0_ffn_gc_b2',
        'L0_ffn_gc_w3', 'L0_ffn_gc_b3', 'L0_ffn_adaptive_range']


def kernel(**inputs):
    import numpy as _np
    import concourse.bacc as _bacc
    from concourse import mybir as _mybir
    from concourse.bass_utils import run_bass_kernel_spmd as _run

    nc = _bacc.Bacc("TRN2", target_bir_lowering=False, num_devices=1)
    arrays, args = {}, []
    for name in _INS:
        a = _np.ascontiguousarray(inputs[name])
        arrays[f"in_{name}_dram"] = a
        args.append(nc.dram_tensor(f"in_{name}_dram", a.shape, _mybir.dt.from_np(a.dtype), kind="ExternalInput").ap())
    args.append(nc.dram_tensor("out_0_dram", (B, S, D), _mybir.dt.float32, kind="ExternalOutput").ap())
    build(nc, *args)
    r = _run(nc, [arrays], core_ids=[0])
    return r.results[0]["out_0_dram"]
```

```python
import concourse.bass as bass
from concourse import mybir
from contextlib import ExitStack

FP32 = mybir.dt.float32
F32R = mybir.dt.float32r
ALU = mybir.AluOpType
ACT = mybir.ActivationFunctionType
AX = mybir.AxisListType

P = 128
B, S, D = 8, 256, 256
H = 16
DK = D // H
C = D // P
TC = S // P
HC = H // C
G = H // 4
SLOT = 32
PARTS = 4 * DK
CYCLES = 3
PAIRS = B // 2
UNITS = CYCLES * PAIRS
TP = 2 * TC
N2 = 2 * S
EPS = 1e-5

STAGES = "ABCD"
STEPS = B + len(STAGES) - 1
LOOP = (4, 8)
LOAD_LOOP = (2, 6)


class At:

    def __init__(self, base, turn=None):
        self.base, self.turn, self.u = base, turn, base % 2

    def n(self):
        return self.base if self.turn is None else self.turn * 2 + self.base

    def back(self, n):
        return At(self.base - n, self.turn)

    def count(self, per, more):
        return per * self.base + more if self.turn is None else self.turn * (2 * per) + (per * self.base + more)

    def count_of_parity(self, per):
        k = self.base // 2 + 1
        return per * k if self.turn is None else self.turn * per + per * k


class Step:
    def __init__(self, base, turn=None):
        self.base, self.turn = base, turn

    def batch(self, stage):
        lag = STAGES.index(stage)
        if self.turn is None and not 0 <= self.base - lag < B:
            return None
        return At(self.base - lag, self.turn)


def run_steps(engine, step, loop=LOOP):
    for s in range(loop[0]):
        step(Step(s))
    with engine.Fori(0, (loop[1] - loop[0]) // 2) as turn:
        for s in range(2):
            step(Step(loop[0] + s, turn))
    for s in range(loop[1], STEPS):
        step(Step(s))


def build(nc, x, ctx_in, g_xattn, g_ffn, wq, bq, wk, bk, wv, bv, wo, bo,
          w1, b1, w2, b2, w3, b3, w4, b4, gw1, gb1, gw2, gb2, gw3, gb3, arange, out):
    with ExitStack() as stack:
        def sb(name, shape, dt=FP32):
            return stack.enter_context(nc.sbuf_tensor(name, shape, dt))

        def sem(name):
            return stack.enter_context(nc.semaphore(name))

        stacks_at = -(-nc.sbuf_base // 32) * 32
        sb("stacks", [P, 4, H, S])
        place = lambda name, i, shape, dt: nc.alloc_sbuf_tensor_at(name, shape, dt, offset=stacks_at + i * H * S * 4)
        q_st = [place(f"q_st{u}", 2 * u, [P, H, S], F32R) for u in range(2)]
        k_st = [place(f"k_st{u}", 2 * u + 1, [P, H, S], F32R) for u in range(2)]
        xr = place("xr", 0, [P, B, TC, D], FP32)
        tw = place("tw", 1, [P, B, TC, D], FP32)
        mixed = place("mixed", 2, [P, PAIRS, TP, D], FP32)
        uv_2 = place("uv_2", 3, [P, TP, 2 * D], FP32)

        ident = sb("ident", [P, P])
        ones = sb("ones", [P, P])
        half_neg = sb("half_neg", [P, TC])
        eps = sb("eps", [P, TC])
        wkv_hi, wkv_lo = (sb(f"wkv_{part}", [P, 2, C, D], F32R) for part in ("hi", "lo"))
        wqo = sb("wqo", [P, 2, C, D])
        w1_sb = sb("w1_sb", [P, C, D])
        w2_sb = sb("w2_sb", [P, C, P])
        w3_sb = sb("w3_sb", [P, 64])
        w4_col = sb("w4_col", [P, 2])
        uv_hi = sb("uv_hi", [P, C, 2 * D], F32R)
        uv_lo = sb("uv_lo", [P, C, 2 * D], F32R)
        gw1_sb = sb("gw1_sb", [P, C, P])
        gw2_sb = sb("gw2_sb", [P, 64])
        gw3_col = sb("gw3_col", [64, 1])
        gw3_rep = sb("gw3_rep", [64, P])
        bqk = sb("bqk", [P, 2, C])
        bv_col = sb("bv_col", [P, C])
        bo_bc = sb("bo_bc", [P, D])
        b1_sb = sb("b1_sb", [P, C])
        b2_sb = sb("b2_sb", [P, 1])
        b3_sb = sb("b3_sb", [P, 1])
        gb1_sb = sb("gb1_sb", [P, 1])
        gb2_sb = sb("gb2_sb", [64, 1])
        scal = sb("scal", [P, 5])
        tanh_g = sb("tanh_g", [P, 2])
        half_b = sb("half_b", [P, 2])
        sign = sb("sign", [P, 2])
        gain = sb("gain", [P, 3])

        x_in = sb("x_in", [P, B, TC, D])
        c_in = sb("c_in", [P, 2, TC, D])
        xn = sb("xn", [P, TC, D])
        x_t = sb("x_t", [P, C, S])
        stats = sb("stats", [P, TC, 6])
        mean_var = sb("mean_var", [P, TC, 2])
        var_eps = sb("var_eps", [P, TC])
        rstd = sb("rstd", [P, TC])
        ct_hi, ct_lo = (sb(f"ct_{part}", [P, 2, C, S], F32R) for part in ("hi", "lo"))
        q_hi = sb("q_hi", [P, 2, C, S], F32R)
        q_lo = sb("q_lo", [P, 2, C, S], F32R)
        k_hi = sb("k_hi", [P, 2, C, S], F32R)
        k_lo = sb("k_lo", [P, 2, C, S], F32R)
        v_sl = sb("v_sl", [P, 2, TC, H, SLOT])
        neg_max = sb("neg_max", [P, C, HC, TC])
        max_parts = sb("max_parts", [P, C, 2, HC, TC], F32R)
        max_t = [sb(f"max_t{c}", [2 * HC * TC, P], F32R) for c in range(C)]
        probs = sb("probs", [P, 2, 4, S])
        o_t = sb("o_t", [P, 2, G, S])
        o_n = sb("o_n", [P, TC, D])
        x_b = sb("x_b", [P, TC, D])
        x2n = sb("x2n", [P, TC, D])
        o_nt = sb("o_nt", [P, C, S])
        rden = sb("rden", [P, TC, 2, 4])
        stats2 = sb("stats2", [P, TC, 6])
        mean_var2 = sb("mean_var2", [P, TC, 2])
        var_eps2 = sb("var_eps2", [P, TC])
        rstd2 = sb("rstd2", [P, TC])
        x2 = sb("x2", [P, B, TC, D])
        w_raw = x2[:, 0:4, :, :]
        mean_all = sb("mean_all", [P, B, TC])
        rstd_all = sb("rstd_all", [P, B, TC])
        state = x_in
        uv_0 = sb("uv_0", [P, TP, 2 * D])
        sums = sb("sums", [P, C, B])

        h1 = [v_sl[:, u, :, :, :].rearrange("p t h e -> p t (h e)") for u in range(2)]
        h2 = [probs[:, 0, 2 * u:2 * u + 2, :].rearrange("p a s -> p (a s)") for u in range(2)]
        h3 = [probs[:, 1, u, :] for u in range(2)]
        uv = [[uv_0[:, k, :] for k in range(TP)],
              [c_in[:, 0, :, :].rearrange("p t d -> p (t d)"), c_in[:, 1, :, :].rearrange("p t d -> p (t d)"),
               xn[:, :, :].rearrange("p t d -> p (t d)"), o_t[:, 0, 0:2, :].rearrange("p g s -> p (g s)")],
              [uv_2[:, k, :] for k in range(TP)],
              [x_in[:, k, :, :].rearrange("p t d -> p (t d)") for k in range(TP)]]
        x_parts = [[t[:, c, :, :] for c in range(C)] for t in (q_hi, q_lo, k_hi, k_lo)]
        x_hi, x_lo = x_parts[0::2], x_parts[1::2]
        tz = sb("tz", [P, UNITS, 2, TC])
        coup = sb("coup", [P, UNITS, 2, TC])
        minus_c1 = sb("minus_c1", [P, PAIRS, 2, TC])
        alpha2 = sb("alpha2", [P, PAIRS, 2, TC])
        beta2 = sb("beta2", [P, PAIRS, 2, TC])
        g_alpha2 = sb("g_alpha2", [P, PAIRS, 2, TC])
        g_beta2 = sb("g_beta2", [P, PAIRS, 2, TC])
        prod = sb("prod", [P, PAIRS, 4, 2, TC])
        gr_beta2 = sb("gr_beta2", [P, PAIRS, 2, TC])
        gr_alpha2 = sb("gr_alpha2", [P, PAIRS, 2, TC])
        gr_alpha3 = sb("gr_alpha3", [P, PAIRS, 2, TC])
        g_beta3 = sb("g_beta3", [P, PAIRS, 2, TC])
        out_scale = sb("out_scale", [P, PAIRS, 2, TC])
        out_shift = sb("out_shift", [P, PAIRS, 2, TC])
        gh1 = sb("gh1", [P, B])
        gh2 = sb("gh2", [64, B])
        gz = sb("gz", [P, B])
        base_c = sb("base_c", [P, B])

        bank = [stack.enter_context(nc.psum_tensor(f"bank{i}", [P, 512], FP32)) for i in range(8)]
        st_bank, s1_bank, pv_bank, misc = bank[0:2], bank[2:4], bank[4:6], bank[6:8]
        l1_bank, uv_bank, l2_bank, l3_bank, l4_bank, gl_bank = bank[0:2], bank[2:4], bank[4], bank[5], bank[6], bank[7]

        names = """ident_done half_neg_done params_in gates_in small_in bias_in w_tp_ready w_t_copied tanh_done
            prep_done gates_ready k0_zeroed k1_zeroed q0_zeroed q1_zeroed w4_zeroed ones_done v_zeroed v_ones aggr_done rstd_added rstd_done xn_done
            c_tp_ready ct_hi_done x_tp_ready x_t_copied
            k_ready k_hi_done k_lo_done q_ready q_hi_done q_lo_done v_ready v_done
            s1_ready s1_maxed max_hi_done max_parts_done max_tp_ready max_t_copied
            st_ready exp_done pv_done o_t_copied o_tp_ready rden_done o_normed o_nt_ready o_nt_copied
            xb_done y_ready x2_done aggr2_done rstd2_added rstd2_done x2n_done x2_tp_ready state_ready
            l1_ready g1_done l2_ready g2_done l3_ready g3_done l4_ready tanh_z_done coup_done
            x_hi_done x_parts_done uv_ready uv_done mixed_done xr_done tw_done gl_ready gl_done base_done fin_done stats_kept
            w_lo_done ct_lo_done bv_repeated wo_bv_ready wo_bv_added out_scaled coefficients_done w1_hi_done""".split()
        sem_of = {n: sem(n) for n in names}
        x_loaded = [sem(f"x_loaded{u}") for u in range(2)]
        c_loaded = [sem(f"c_loaded{u}") for u in range(2)]
        stacked = [[sem(f"stacked{u}{c}") for c in range(C)] for u in range(2)]
        max_stored = [[sem(f"max_stored{u}{c}") for c in range(C)] for u in range(2)]
        weight_in = [sem(f"weight_in{i}") for i in range(4)]
        ones_stored = [sem(f"ones_stored{u}") for u in range(2)]
        stored = sem("stored")
        (ident_done, half_neg_done, params_in, gates_in, small_in, bias_in, w_tp_ready, w_t_copied, tanh_done,
         prep_done, gates_ready, k0_zeroed, k1_zeroed, q0_zeroed, q1_zeroed, w4_zeroed, ones_done, v_zeroed, v_ones, aggr_done, rstd_added, rstd_done, xn_done,
         c_tp_ready, ct_hi_done, x_tp_ready, x_t_copied,
         k_ready, k_hi_done, k_lo_done, q_ready, q_hi_done, q_lo_done, v_ready, v_done,
         s1_ready, s1_maxed, max_hi_done, max_parts_done, max_tp_ready, max_t_copied,
         st_ready, exp_done, pv_done, o_t_copied, o_tp_ready, rden_done, o_normed, o_nt_ready, o_nt_copied,
         xb_done, y_ready, x2_done, aggr2_done, rstd2_added, rstd2_done, x2n_done, x2_tp_ready,
         state_ready, l1_ready, g1_done, l2_ready, g2_done, l3_ready, g3_done, l4_ready, tanh_z_done, coup_done,
         x_hi_done, x_parts_done, uv_ready, uv_done, mixed_done, xr_done, tw_done, gl_ready, gl_done, base_done, 
         fin_done, stats_kept, w_lo_done, ct_lo_done, bv_repeated, wo_bv_ready, wo_bv_added, out_scaled, coefficients_done, w1_hi_done) = [sem_of[n] for n in names]

        USES = [
            [("max1", "C", max_t_copied, 2, 2), ("o_a", "D", o_normed, 2, 1), ("o_b", "D", o_normed, 2, 2),
             ("o_nt", "D", o_nt_copied, 1, 1), ("y", "D", x2_done, 1, 1), ("max0", "B", max_t_copied, 2, 1), ("x2_t", "D", state_ready, 2, 2)],
            [("c_t", "A", ct_lo_done, 1, 1), ("k", "A", k_lo_done, 2, 2), ("x_t", "A", x_t_copied, 1, 1),
             ("q", "A", q_lo_done, 2, 2), ("v", "B", v_done, 1, 1)],
        ]

        def free_bank(pe, step, use):
            m = 0 if any(u[0] == use for u in USES[0]) else 1
            order = USES[m]
            i = [u[0] for u in order].index(use)
            for back in range(1, 2 * len(order) + 1):
                name, stage, signal, per, more = order[(i - back) % len(order)]
                ago = Step(step.base - (0 if back <= i else 1 if back <= i + len(order) else 2), step.turn)
                at = ago.batch(stage)
                if at is not None:
                    pe.wait_ge(signal, at.count(per, more))
                    break
            return misc[m]

        def query_bank(a):
            return misc[0] if a.turn is None and a.base < 2 else misc[1]

        def uv_work(st, j):
            if st.turn is not None or st.base < B + 1:
                return None
            pair, part = divmod((st.base - B - 1) * 8 + j, TP + 1)
            return (pair, part - 1 if part else None)

        weight_bank = [pv_bank[0], pv_bank[1], st_bank[0], st_bank[1]]

        def weight_rows(psum, w):
            src = psum[:, :].rearrange("p (a n) -> p a n", a=2 * C)
            return src.rearrange("p a (h r) -> p a h r", r=DK) if w < 2 else src

        def weight_columns(part, w):
            dst = part[:, w // 2, :, :].rearrange("p a (c n) -> p (a c) n", c=C)
            return dst.rearrange("p a (r h) -> p a h r", r=DK) if w < 2 else dst

        W_ORDER = (1, 0, 2, 3)
        block = stack.enter_context(nc.Block())

        @block.sync
        def _(sp):
            def load(at):
                if at.turn is not None or at.base >= 2:
                    sp.wait_ge(xn_done, at.back(2).count(1, 1))
                    sp.wait_ge(c_tp_ready, at.back(2).count(1, 1))
                b = bass.ds(at.n(), 1)
                sp.dma_start(c_in[:, at.u, :, :],
                             ctx_in[b, :, :].rearrange("b (t p) d -> p (b t) d", p=P)).then_inc(c_loaded[at.u], 16)
                sp.dma_start(x_in[:, b, :, :].rearrange("p b t d -> p (b t) d"),
                             x[b, :, :].rearrange("b (t p) d -> p (b t) d", p=P)).then_inc(x_loaded[at.u], 16)

            def stack_parts(at, c):
                first = at.turn is None and at.base < 2
                heads = slice(c * HC, (c + 1) * HC)
                if c == 1:
                    if not first:
                        sp.wait_ge(st_ready, at.back(2).count(16, 16))
                elif first:
                    sp.wait_ge(k_lo_done, at.count(2, 2))
                else:
                    sp.wait_ge(q_lo_done, at.count(2, 2))
                for i, k_part in enumerate((k_hi, k_hi, k_lo, k_lo)):
                    sp.dma_start(k_st[at.u][i * DK:(i + 1) * DK, heads, :].bitcast(FP32),
                                 k_part[:, at.u, c, :].bitcast(FP32)).then_inc(stacked[at.u][c], 16)
                if c == 0 and first:
                    sp.wait_ge(q_lo_done, at.count(2, 2))
                    sp.wait_ge((q0_zeroed, q1_zeroed)[at.u], 1)
                for i, q_part in enumerate((q_hi, q_lo, q_hi, q_lo)):
                    sp.dma_start(q_st[at.u][i * DK:(i + 1) * DK, heads, :].bitcast(FP32),
                                 q_part[:, at.u, c, :].bitcast(FP32)).then_inc(stacked[at.u][c], 16)
                sp.dma_start(q_st[at.u][PARTS:PARTS + 2, heads, :].bitcast(FP32),
                             k_st[0][PARTS + 2:PARTS + 4, 0:HC, :].bitcast(FP32)).then_inc(stacked[at.u][c], 16)

            def store_max(at, c):
                sp.wait_ge(max_t_copied, at.count(2, c + 1))
                sp.dma_start(q_st[at.u][PARTS:PARTS + 2, c * HC:(c + 1) * HC, :].bitcast(FP32),
                             max_t[c][:, :].bitcast(FP32)).then_inc(max_stored[at.u][c], 16)

            load(At(0))
            for i, bias in enumerate((bq, bk)):
                for c in range(C):
                    sp.dma_start(bqk[:, i, c:c + 1], bias[c * P:(c + 1) * P].rearrange("(h r a) -> r h a", r=DK, a=1),
                                  allow_slow_non_contiguous=True).then_inc(bias_in, 16)
            for c in range(C):
                sp.dma_start(bv_col[:, c:c + 1], bv[c * P:(c + 1) * P].rearrange("(p a) -> p a", a=1),
                             allow_slow_non_contiguous=True).then_inc(bias_in, 16)
            for w, i in ((wv, 2), (wo, 3)):
                sp.dma_start(w_raw[:, i, :, :], w.rearrange("(c p) i -> p c i", p=P)).then_inc(weight_in[i], 16)
            load(At(1))
            def store_ones(u):
                sp.wait_ge((k0_zeroed, k1_zeroed)[u], 1)
                sp.dma_start(k_st[u][PARTS:PARTS + 2, :, :].bitcast(FP32), ones[0:2 * H * S // P, :]).then_inc(ones_stored[u], 16)

            sp.wait_ge(ones_done, 1)
            store_ones(0)
            store_ones(1)

            def load_params():
                sp.dma_start(w1_sb[:, :, :], w1.rearrange("(c p) i -> p c i", p=P)).then_inc(params_in, 16)
                sp.dma_start(w2_sb[:, :, :], w2.rearrange("(c p) i -> p c i", p=P)).then_inc(params_in, 16)
                sp.dma_start(w3_sb[:, :], w3).then_inc(params_in, 16)
                sp.dma_start(gw1_sb[:, :, :], gw1.rearrange("(c p) i -> p c i", p=P)).then_inc(params_in, 16)
                sp.dma_start(gw2_sb[:, :], gw2).then_inc(params_in, 16)

            def step(st):
                a, b, c = st.batch("A"), st.batch("B"), st.batch("C")
                if st.turn is None and st.base < 2:
                    sp.wait_ge(ones_stored[st.base], 16)
                if c:
                    store_max(c, 1)
                if a:
                    stack_parts(a, 0)
                if b:
                    store_max(b, 0)
                if st.turn is not None or st.base + 2 < B:
                    load(At(st.base + 2, st.turn))
                if a:
                    stack_parts(a, 1)
                if st.turn is None and st.base == 1:
                    load_params()

            run_steps(sp, step, LOAD_LOOP)

            for i, b in enumerate((*range(B - 2), B - 1, B - 2)):
                sp.wait_ge(fin_done, TC * (i + 1))
                sp.dma_start(out[b, :, :].rearrange("(t p) d -> p t d", p=P), x2[:, b, :, :]).then_inc(stored, 16)
            sp.wait_ge(stored, 16 * B)

        @block.gpsimd
        def _(pool):
            nc.gpsimd.memset(ident[:, :], 0.0).then_inc(ident_done, 1)
            pool.wait_ge(ident_done, 1)
            nc.gpsimd.affine_select(out=ident[:, :], in_=ident[:, :], compare_op=ALU.not_equal, fill=1.0,
                                    base=0, pattern=[[-1, P]], channel_multiplier=1).then_inc(ident_done, 1)
            nc.gpsimd.memset(half_neg[:, :], -0.5).then_inc(half_neg_done, 1)
            nc.gpsimd.memset(eps[:, :], EPS).then_inc(half_neg_done, 1)
            pool.wait_ge(half_neg_done, 2)
            nc.gpsimd.memset(k_st[0][64:P, :, :].bitcast(FP32), 0.0).then_inc(k0_zeroed, 1)
            pool.wait_ge(k0_zeroed, 1)

            def load_small(pairs, done):
                for dst, src in pairs:
                    pool.dma_start(dst, src, allow_slow_non_contiguous=True).then_inc(done, 16)

            def zero_rest():
                pool.wait_ge(rstd_done, 1)
                nc.gpsimd.memset(q_st[0][64:P, :, :].bitcast(FP32), 0.0).then_inc(q0_zeroed, 1)
                pool.wait_ge(q0_zeroed, 1)
                nc.gpsimd.memset(w4_col[:, :], 0.0).then_inc(w4_zeroed, 1)
                pool.wait_ge(w4_zeroed, 1)
                nc.gpsimd.memset(q_st[1][64:P, :, :].bitcast(FP32), 0.0).then_inc(q1_zeroed, 1)
                pool.wait_ge(q1_zeroed, 1)
                nc.gpsimd.memset(v_sl[:, :, :, :, DK:SLOT].rearrange("p u t h e -> p (u t h) e"), 0.0).then_inc(v_zeroed, 1)
                pool.wait_ge(v_zeroed, 1)
                nc.gpsimd.memset(v_sl[:, :, :, :, DK:DK + 1].rearrange("p u t h e -> p (u t h) e"), 1.0).then_inc(v_ones, 1)
                pool.wait_ge(v_ones, 1)

            def load_gates():
                load_small(((bo_bc[:, :], bo.partition_broadcast(P)),
                            (scal[:, 0:1], g_xattn.partition_broadcast(P)),
                            (scal[:, 1:2], g_ffn.partition_broadcast(P)),
                            (scal[:, 2:3], arange.partition_broadcast(P)),
                            (scal[:, 3:4], b4.partition_broadcast(P)),
                            (scal[:, 4:5], gb3.partition_broadcast(P))), gates_in)

            def load_ffn():
                load_small(((b1_sb[:, 0:1], b1[0:P].rearrange("(p a) -> p a", a=1)),
                            (b1_sb[:, 1:2], b1[P:D].rearrange("(p a) -> p a", a=1)),
                            (b2_sb[:, :], b2.rearrange("(p a) -> p a", a=1)),
                            (b3_sb[0:64, :], b3.rearrange("(p a) -> p a", a=1)),
                            (b3_sb[64:P, :], b3.rearrange("(p a) -> p a", a=1)),
                            (gb1_sb[:, :], gb1.rearrange("(p a) -> p a", a=1)),
                            (gb2_sb[:, :], gb2.rearrange("(p a) -> p a", a=1)),
                            (gw3_col[:, :], gw3),
                            (w4_col[0:64, 0:1], w4),
                            (w4_col[64:P, 1:2], w4)), small_in)

            def step(st):
                a, d = st.batch("A"), st.batch("D")
                if a:
                    pool.wait_ge(aggr_done, a.count(2, 2))
                    nc.gpsimd.tensor_tensor(var_eps[:, :], mean_var[:, :, 1], eps[:, :], ALU.add).then_inc(rstd_added, 1)
                    pool.wait_ge(rstd_added, a.count(1, 1))
                    if a.turn is not None or a.base >= 1:
                        pool.wait_ge(xn_done, a.count(1, 0))
                    nc.gpsimd.tensor_tensor(rstd[:, :], var_eps[:, :], half_neg[:, :], ALU.pow).then_inc(rstd_done, 1)
                if d:
                    pool.wait_ge(gates_ready, 1)
                    if d.turn is not None or d.base >= 1:
                        pool.wait_ge(x2_done, d.count(1, 0))
                    b = bass.ds(d.n(), 1)
                    for t in range(TC):
                        ins = nc.gpsimd.tensor_tensor(x_b[:, t, :], x_in[:, b, t, :].rearrange("p b d -> p (b d)"),
                                                      bo_bc[:, :], ALU.add)
                        ins.then_inc(xb_done, 1)
                    pool.wait_ge(aggr2_done, d.count(2, 2))
                    nc.gpsimd.tensor_tensor(var_eps2[:, :], mean_var2[:, :, 1], eps[:, :], ALU.add).then_inc(rstd2_added, 1)
                    pool.wait_ge(rstd2_added, d.count(1, 1))
                    nc.gpsimd.tensor_tensor(rstd2[:, :], var_eps2[:, :], half_neg[:, :], ALU.pow).then_inc(rstd2_done, 1)
                if st.turn is None and st.base < 3:
                    (zero_rest, load_gates, load_ffn)[st.base]()

            run_steps(pool, step)

            Q = D // 4
            pool.wait_ge(st_ready, 16 * (B - 1))

            def unfold(b):
                pool.wait_ge(stats_kept, b + 1)
                for t in range(TC):
                    last = nc.gpsimd.tensor_scalar(xr[:, b, t, :], x2[:, b, t, :], mean_all[:, b, t:t + 1],
                                                   rstd_all[:, b, t:t + 1], ALU.subtract, ALU.mult)
                last.then_inc(xr_done, 1)
                pool.wait_ge(xr_done, b + 1)
                for to, of, factor in ((0, 2, 1.0), (1, 3, -1.0), (2, 0, -1.0), (3, 1, 1.0)):
                    last = nc.gpsimd.tensor_scalar(tw[:, b, :, to * Q:(to + 1) * Q], xr[:, b, :, of * Q:(of + 1) * Q],
                                                   factor, None, ALU.mult)
                last.then_inc(tw_done, 1)

            for b in range(B):
                unfold(b)

        @block.tensor
        def _(pe):
            pe.wait_ge(ident_done, 2)

            def transpose_weight(i, psum):
                w = W_ORDER[i]
                pe.wait_ge(weight_in[w], 16)
                for ci in range(C):
                    for co in range(C):
                        last = nc.tensor.transpose(psum[:, ci * D + co * P:ci * D + (co + 1) * P],
                                                   w_raw[:, w, co, ci * P:(ci + 1) * P], ident[:, :])
                last.then_inc(w_tp_ready, 1)

            for i in range(2):
                transpose_weight(i, weight_bank[i])

            def transposes(psum, src, ready):
                for c in range(C):
                    for t in range(TC):
                        last = nc.tensor.transpose(psum[:, c * S + t * P:c * S + (t + 1) * P],
                                                   src[:, t, c * P:(c + 1) * P], ident[:, :])
                last.then_inc(ready, 1)

            def product(psum, pairs):
                for i, (lhs_t, rhs) in enumerate(pairs):
                    last = nc.tensor.matmul(psum, lhs_t, rhs, start=(i == 0), stop=(i == len(pairs) - 1))
                return last

            def times_kv(src, w):
                return [(s_part[:, ci, :], w_part[:, w, ci, :]) for s_part, w_part in
                        ((src[0], wkv_hi), (src[0], wkv_lo), (src[1], wkv_hi)) for ci in range(C)]

            def times_qo(src, w):
                return [(src[:, ci, :], wqo[:, w, ci, :]) for ci in range(C)]

            def project(psum, pairs, ready):
                for co in range(C):
                    last = product(psum[:, co * S:(co + 1) * S], [(w[:, co * P:(co + 1) * P], src) for src, w in pairs])
                last.then_inc(ready, 1)

            def project_rows(psum, pairs, ready):
                for t in range(TC):
                    last = product(psum[:, t * D:(t + 1) * D], [(src[:, t * P:(t + 1) * P], w) for src, w in pairs])
                last.then_inc(ready, 1)

            def scores_max_pass(b, j):
                if j % 4 == 0:
                    c = j // 4
                    pe.wait_ge(stacked[b.u][c], b.count_of_parity(16 * 9))
                for t in range(TC):
                    n = 2 * j + t
                    if b.turn is not None or b.base > 0 or n >= 2:
                        pe.wait_ge(s1_maxed, b.count(16, n - 1))
                    for i in range(2):
                        h = 2 * j + i
                        last = nc.tensor.matmul(s1_bank[t][:, i * S:(i + 1) * S],
                                                q_st[b.u][:, h, t * P:(t + 1) * P], k_st[b.u][:, h, :],
                                                start=True, stop=True)
                    last.then_inc(s1_ready, 1)

            def scores_exp_pass(c, j):
                g, t = j // 2, j % 2
                if j % 4 == 0:
                    pe.wait_ge(max_stored[c.u][j // 4], c.count_of_parity(16))
                for i in range(2):
                    n = 2 * j + i
                    if c.turn is not None or c.base > 0 or n >= 2:
                        pe.wait_ge(exp_done, c.count(16, n - 1))
                    for e in range(2):
                        h = 4 * g + 2 * i + e
                        last = nc.tensor.matmul(st_bank[i][:, e * S:(e + 1) * S],
                                                k_st[c.u][:, h, t * P:(t + 1) * P], q_st[c.u][:, h, :],
                                                start=True, stop=True)
                    last.then_inc(st_ready, 1)

            def times_values(c, j):
                g, t = j // 2, j % 2
                pe.wait_ge(exp_done, c.count(16, 2 * j + 2))
                if j == 0:
                    pe.wait_ge(v_done, c.count(1, 1))
                if t == 0 and (c.turn is not None or c.base > 0 or g >= 2):
                    pe.wait_ge(o_t_copied, c.count(4, g - 1))
                for i in range(4):
                    last = nc.tensor.matmul(pv_bank[g % 2][SLOT * i:SLOT * (i + 1), 0:S],
                                            v_sl[:, c.u, t, 4 * g + i, :], probs[:, j % 2, i, :],
                                            start=(t == 0), stop=(t == TC - 1))
                last.then_inc(pv_done, 1)

            def transpose_max(st, at, c):
                pe.wait_ge(max_parts_done, at.count(2, c + 1))
                psum = free_bank(pe, st, f"max{c}")
                nc.tensor.transpose(psum[0:2 * HC * TC, 0:P],
                                    max_parts[:, c, :, :, :].bitcast(FP32).rearrange("p a h t -> p (a h t)"),
                                    ident[:, :]).then_inc(max_tp_ready, 1)

            def transpose_outputs(st, d, half):
                pe.wait_ge(o_t_copied, d.count(4, 2 * half + 2))
                psum = free_bank(pe, st, "o_a" if half == 0 else "o_b")
                for t in range(TC):
                    for i in range(2):
                        last = nc.tensor.transpose(psum[:, (2 * t + i) * P:(2 * t + i + 1) * P],
                                                   o_t[:, d.u, 2 * half + i, t * P:(t + 1) * P], ident[:, :])
                last.then_inc(o_tp_ready, 1)

            def products(p, k):
                n = TP * p + k
                if n == 0:
                    pe.wait_ge(s1_maxed, 16 * B)
                if k == 0:
                    pe.wait_ge(x_parts_done, 2 * (p + 1))
                if n >= 2:
                    pe.wait_ge(uv_done, n - 1)
                i = 0
                for x_part, w_part in ((x_hi, uv_hi), (x_hi, uv_lo), (x_lo, uv_hi)):
                    for ci in range(C):
                        last = nc.tensor.matmul(uv_bank[n % 2][:, :], x_part[p % 2][ci][:, k // TC, k % TC * P:(k % TC + 1) * P],
                                                w_part[:, ci, :], start=(i == 0), stop=(i == 3 * C - 1))
                        i += 1
                last.then_inc(uv_ready, 1)

            def layer1(n):
                p = n % PAIRS
                if n < PAIRS:
                    pe.wait_ge(uv_done, TP * (p + 1))
                    src = lambda k: uv[p][k]
                else:
                    pe.wait_ge(mixed_done, n - PAIRS + 1)
                    src = lambda k: mixed[:, p, k, :]
                if n >= 1:
                    pe.wait_ge(g1_done, 2 * n)
                for co in range(C):
                    for k in range(TP):
                        last = nc.tensor.transpose(l1_bank[co][:, k * P:(k + 1) * P], src(k)[:, co * P:(co + 1) * P],
                                                   ident[:, :])
                    last.then_inc(l1_ready, 1)

            def layer2(n):
                pe.wait_ge(g1_done, 2 * n + 2)
                if n >= 1:
                    pe.wait_ge(g2_done, n)
                for ci in range(C):
                    last = nc.tensor.matmul(l2_bank[:, :], w2_sb[:, ci, :], h1[n % 2][:, ci, :],
                                            start=(ci == 0), stop=(ci == C - 1))
                last.then_inc(l2_ready, 1)

            def layer3(n):
                pe.wait_ge(g2_done, n + 1)
                if n >= 1:
                    pe.wait_ge(g3_done, n)
                for half in range(2):
                    last = nc.tensor.matmul(l3_bank[64 * half:64 * (half + 1), 0:S], w3_sb[:, :],
                                            h2[n % 2][:, half * S:(half + 1) * S], start=True, stop=True)
                last.then_inc(l3_ready, 1)

            def layer4(n):
                pe.wait_ge(g3_done, n + 1)
                if n >= 1:
                    pe.wait_ge(tanh_z_done, n)
                for t in range(TC):
                    last = nc.tensor.matmul(l4_bank[:, 2 * t:2 * t + 2], h3[n % 2][:, t * P:(t + 1) * P], w4_col[:, :],
                                            start=True, stop=True)
                last.then_inc(l4_ready, 1)

            def first_projections(a):
                pe.wait_ge(c_loaded[0], 16)
                transposes(misc[1], c_in[:, 0, :, :], c_tp_ready)
                pe.wait_ge(w_lo_done, 1)
                pe.wait_ge(ct_lo_done, 1)
                project(misc[1], times_kv((ct_hi[:, 0, :, :], ct_lo[:, 0, :, :]), 0), k_ready)
                pe.wait_ge(xn_done, 1)
                transposes(query_bank(a), xn, x_tp_ready)
                pe.wait_ge(w_t_copied, 2)
                pe.wait_ge(x_t_copied, 1)
                project(query_bank(a), times_qo(x_t, 0), q_ready)
                for i in range(2, 4):
                    transpose_weight(i, weight_bank[i])

            def output_bias():
                pe.wait_ge(bv_repeated, C)
                pe.wait_ge(max_t_copied, 2 * 1 + 1)
                product(misc[0][:, 0:D], [(x2n[:, ci, 0:P], wqo[:, 1, ci, :]) for ci in range(C)]
                        ).then_inc(wo_bv_ready, 1)

            def project_k(st, a):
                pe.wait_ge(ct_lo_done, a.count(1, 1))
                project(free_bank(pe, st, "k"), times_kv((ct_hi[:, a.u, :, :], ct_lo[:, a.u, :, :]), 0), k_ready)

            def transpose_x(st, a):
                pe.wait_ge(xn_done, a.count(1, 1))
                if query_bank(a) is misc[1]:
                    free_bank(pe, st, "x_t")
                else:
                    pe.wait_ge(q_lo_done, a.count(2, 0))
                transposes(query_bank(a), xn, x_tp_ready)

            def step(st):
                a, b, c, d = (st.batch(x) for x in STAGES)
                if st.turn is None and st.base == 0:
                    first_projections(a)
                    return
                early = st.turn is None and st.base == 1
                for j in range(8):
                    if c:
                        scores_exp_pass(c, j)
                    if j == 0 and d:
                        times_values(d, 7)
                    if j > 0 and c:
                        times_values(c, j - 1)
                    if j == 0 and a:
                        pe.wait_ge(c_loaded[a.u], a.count_of_parity(16))
                        transposes(free_bank(pe, st, "c_t"), c_in[:, a.u, :, :], c_tp_ready)
                    if j == 0 and early:
                        project_k(st, a)
                        transpose_x(st, a)
                    if j == 1 and c:
                        if st.turn is None and st.base == 3:
                            pe.wait_ge(wo_bv_added, 1)
                        transpose_max(st, c, 1)
                    if j == 7 and d:
                        pe.wait_ge(x2n_done, d.count(1, 1))
                        transposes(free_bank(pe, st, "x2_t"), x2n, x2_tp_ready)
                    if b:
                        scores_max_pass(b, j)
                    if j == 1:
                        if d:
                            transpose_outputs(st, d, 0)
                        if a and not early:
                            project_k(st, a)
                    if j == 2:
                        if d:
                            transpose_outputs(st, d, 1)
                        if a and not early:
                            transpose_x(st, a)
                    if j == (0 if early else 3) and a:
                        pe.wait_ge(x_t_copied, a.count(1, 1))
                        if query_bank(a) is misc[1]:
                            free_bank(pe, st, "q")
                        project(query_bank(a), times_qo(x_t, 0), q_ready)
                    if j == 3:
                        if d:
                            pe.wait_ge(o_normed, d.count(2, 2))
                            transposes(free_bank(pe, st, "o_nt"), o_n, o_nt_ready)
                    if j == 4 and d:
                        pe.wait_ge(o_nt_copied, d.count(1, 1))
                        project_rows(free_bank(pe, st, "y"), times_qo(o_nt, 1), y_ready)
                    if j == 5 and b:
                        if early:
                            pe.wait_ge(q_lo_done, 2 * 2)
                        transpose_max(st, b, 0)
                    if j == 5 and b:
                        if b.turn is None and b.base == 0:
                            pe.wait_ge(w_t_copied, 4)
                            pe.wait_ge(w_lo_done, 2)
                        pe.wait_ge(ct_lo_done, b.count(1, 1))
                        project_rows(free_bank(pe, st, "v"), times_kv((ct_hi[:, b.u, :, :], ct_lo[:, b.u, :, :]), 1), v_ready)
                    work = uv_work(st, j)
                    if work and work[1] is not None:
                        products(*work)
                    if j == 2 and st.turn is None and st.base == STEPS - 1:
                        pe.wait_ge(exp_done, 16 * B)
                        layer1(0)
                if st.turn is None and st.base == 2:
                    output_bias()

            run_steps(pe, step)

            last_pair = PAIRS - 1
            pe.wait_ge(o_t_copied, 4 * B)
            layer2(0)
            pe.wait_ge(state_ready, 2 * B)
            for ci in range(C):
                last = nc.tensor.matmul(gl_bank[:, 0:B], gw1_sb[:, ci, :], sums[:, ci, :],
                                        start=(ci == 0), stop=(ci == C - 1))
            last.then_inc(gl_ready, 1)
            layer1(1)
            products(last_pair, 0)
            pe.wait_ge(gl_done, 1)
            nc.tensor.matmul(gl_bank[0:64, 64:64 + B], gw2_sb[:, :], gh1[:, :], start=True, stop=True).then_inc(gl_ready, 1)
            products(last_pair, 1)
            pe.wait_ge(gl_done, 2)
            nc.tensor.matmul(gl_bank[:, 128:128 + B], gw3_rep[:, :], gh2[:, :], start=True, stop=True).then_inc(gl_ready, 1)
            products(last_pair, 2)
            products(last_pair, 3)
            for n in range(2, UNITS + 2):
                if n < UNITS:
                    layer1(n)
                if n == UNITS:
                    layer2(n - 1)
                layer3(n - 2)
                if n < UNITS:
                    layer2(n - 1)
                layer4(n - 2)

        @block.scalar
        def _(act):
            for i, w in ((1, wk), (0, wq)):
                act.dma_start(w_raw[:, i, :, :], w.rearrange("(c p) i -> p c i", p=P)).then_inc(weight_in[i], 16)

            def copy_weight(i, psum):
                w = W_ORDER[i]
                act.wait_ge(w_tp_ready, i + 1)
                nc.scalar.copy(weight_columns(wkv_hi if w in (1, 2) else wqo, w), weight_rows(psum, w)).then_inc(w_t_copied, 1)

            for i in range(2):
                copy_weight(i, weight_bank[i])

            def split_hi(p):
                act.wait_ge(state_ready, 2 * (2 * p + 2))
                if p < 2:
                    for c in range(C):
                        act.wait_ge(stacked[0][c], 16 * 9 * (B // 2))
                        act.wait_ge(stacked[1][c], 16 * 9 * (B // 2))
                else:
                    act.wait_ge(uv_ready, TP * (p - 1))
                for ci in range(C):
                    nc.scalar.copy(x_hi[p % 2][ci], state[:, 2 * p:2 * p + 2, ci, :]).then_inc(x_hi_done, 1)

            def copy_uv(p, k):
                act.wait_ge(uv_ready, TP * p + k + 1)
                nc.scalar.copy(uv[p][k], uv_bank[k % 2][:, :]).then_inc(uv_done, 1)

            def project_hi(at, i, dst, ready, done, psum):
                if at.turn is None and at.base == 0 and i == 1:
                    act.wait_ge(bias_in, 16 * 6)
                act.wait_ge(ready, at.count(1, 1))
                for c in range(C):
                    nc.scalar.activation(dst[:, at.u, c, :], psum[:, c * S:(c + 1) * S], ACT.Identity,
                                         bias=bqk[:, i, c:c + 1]).then_inc(done, 1)

            def gelu1(n):
                for co in range(C):
                    act.wait_ge(l1_ready, 2 * n + co + 1)
                    if co == 0 and n >= 2:
                        act.wait_ge(l2_ready, n - 1)
                    nc.scalar.activation(h1[n % 2][:, co, :], l1_bank[co][:, :], ACT.Gelu,
                                         bias=b1_sb[:, co:co + 1]).then_inc(g1_done, 1)

            def gelu2(n):
                act.wait_ge(l2_ready, n + 1)
                if n >= 2:
                    act.wait_ge(l3_ready, n - 1)
                nc.scalar.activation(h2[n % 2], l2_bank[:, :], ACT.Gelu, bias=b2_sb[:, :]).then_inc(g2_done, 1)

            def gelu3(n):
                act.wait_ge(l3_ready, n + 1)
                if n >= 2:
                    act.wait_ge(l4_ready, n - 1)
                nc.scalar.activation(h3[n % 2], l3_bank[:, 0:S], ACT.Gelu, bias=b3_sb[:, :]).then_inc(g3_done, 1)

            def scale_residual(b):
                p, half = divmod(b, 2)
                act.wait_ge(coefficients_done, p + 1)
                act.wait_ge(tw_done, b + 1)
                for t in range(TC):
                    nc.scalar.activation(x2[:, b, t, :], x2[:, b, t, :], ACT.Identity, bias=out_shift[:, p, half, t:t + 1],
                                         scale=out_scale[:, p, half, t:t + 1]).then_inc(out_scaled, 1)

            def tanh_z(n):
                act.wait_ge(l4_ready, n + 1)
                nc.scalar.activation(tz[:, n, :, :].rearrange("p h t -> p t h"),
                                     l4_bank[:, 0:2 * TC].rearrange("p (t h) -> p t h", h=2), ACT.Tanh,
                                     bias=half_b[:, 0:1], scale=0.5).then_inc(tanh_z_done, 1)

            def copy_x_t(a):
                act.wait_ge(x_tp_ready, a.count(1, 1))
                nc.scalar.copy(x_t[:, :, :].rearrange("p c s -> p (c s)"), query_bank(a)[:, :]).then_inc(x_t_copied, 1)

            def copy_max(at, c, m):
                act.wait_ge(max_tp_ready, at.count(2, c + 1))
                if at.turn is not None or at.base >= 1:
                    last = at.back(1)
                    act.wait_ge(max_stored[last.u][c], last.count_of_parity(16))
                nc.scalar.copy(max_t[c][:, :], misc[m][0:2 * HC * TC, 0:P]).then_inc(max_t_copied, 1)

            def copy_outputs(at, g):
                act.wait_ge(pv_done, at.count(8, 2 * g + 2))
                nc.scalar.copy(o_t[:, at.u, g, :], pv_bank[g % 2][:, 0:S]).then_inc(o_t_copied, 1)

            def step(st):
                a, b, c, d = (st.batch(x) for x in STAGES)
                for j in range(8):
                    if c:
                        for i in range(2):
                            act.wait_ge(st_ready, c.count(16, 2 * j + i + 1))
                            if i == 0 and (c.turn is not None or c.base > 0 or j >= 2):
                                act.wait_ge(pv_done, c.count(8, j - 1))
                            nc.scalar.activation(probs[:, j % 2, 2 * i:2 * i + 2, :].rearrange("p e s -> p (e s)"),
                                                 st_bank[i][:, :], ACT.Exp, scale=DK ** -0.5).then_inc(exp_done, 1)
                    if j == 0 and d:
                        copy_outputs(d, 3)
                    if j == 0 and a:
                        act.wait_ge(c_tp_ready, a.count(1, 1))
                        nc.scalar.copy(ct_hi[:, a.u, :, :].rearrange("p c s -> p (c s)"), misc[1][:, :]).then_inc(ct_hi_done, 1)
                    if j == 1 and c:
                        copy_max(c, 1, 0)
                    if j == 1 and a:
                        project_hi(a, 1, k_hi, k_ready, k_hi_done, misc[1])
                    if j == 2 and a:
                        copy_x_t(a)
                    if j == 2 and c:
                        copy_outputs(c, 0)
                    if j == 3 and a:
                        project_hi(a, 0, q_hi, q_ready, q_hi_done, query_bank(a))
                    if j == 3 and d:
                        act.wait_ge(o_nt_ready, d.count(1, 1))
                        nc.scalar.copy(o_nt[:, :, :].rearrange("p c s -> p (c s)"), misc[0][:, :]).then_inc(o_nt_copied, 1)
                    if j == 4 and c:
                        copy_outputs(c, 1)
                    if j == 5 and b:
                        copy_max(b, 0, 0)
                    if j == 6 and c:
                        copy_outputs(c, 2)
                    if j == 6 and b:
                        act.wait_ge(v_ready, b.count(1, 1))
                        if b.turn is None and b.base == 0:
                            act.wait_ge(v_ones, 1)
                        nc.scalar.copy(v_sl[:, b.u, :, :, 0:DK], misc[1][:, :].rearrange("p (t h e) -> p t h e", t=TC, e=DK)
                                       ).then_inc(v_done, 1)
                    if j == 7 and d:
                        act.wait_ge(x2_tp_ready, d.count(1, 1))
                        for ci in range(C):
                            nc.scalar.activation(state[:, bass.ds(d.n(), 1), ci, :].rearrange("p b s -> p (b s)"),
                                                 misc[0][:, ci * S:(ci + 1) * S], ACT.Identity,
                                                 accum_out=sums[:, ci, bass.ds(d.n(), 1)]).then_inc(state_ready, 1)
                    work = uv_work(st, j)
                    if work:
                        (split_hi(work[0]) if work[1] is None else copy_uv(*work))
                    if j == 2 and st.turn is None and st.base == STEPS - 1:
                        act.wait_ge(prep_done, 1)
                        gelu1(0)
                if st.turn is None and st.base == 0:
                    for i in range(2, 4):
                        copy_weight(i, weight_bank[i])
                if st.turn is None and st.base == 2:
                    act.wait_ge(gates_in, 16 * 6)
                    nc.scalar.activation(tanh_g[:, :], scal[:, 0:2], ACT.Tanh).then_inc(tanh_done, 1)

            run_steps(act, step)

            gelu2(0)
            act.wait_ge(gl_ready, 1)
            nc.scalar.activation(gh1[:, :], gl_bank[:, 0:B], ACT.Gelu, bias=gb1_sb[:, :], scale=1.0 / S).then_inc(gl_done, 1)
            gelu1(1)
            copy_uv(PAIRS - 1, 0)
            act.wait_ge(gl_ready, 2)
            nc.scalar.activation(gh2[:, :], gl_bank[0:64, 64:64 + B], ACT.Gelu, bias=gb2_sb[:, :]).then_inc(gl_done, 1)
            copy_uv(PAIRS - 1, 1)
            act.wait_ge(gl_ready, 3)
            nc.scalar.activation(gz[:, :], gl_bank[:, 128:128 + B], ACT.Tanh, bias=half_b[:, 1:2], scale=0.5).then_inc(gl_done, 1)
            for k in range(2, TP):
                copy_uv(PAIRS - 1, k)
            for n in range(2, UNITS + 2):
                if n < UNITS:
                    gelu1(n)
                if n == UNITS:
                    gelu2(n - 1)
                gelu3(n - 2)
                if n < UNITS:
                    gelu2(n - 1)
                if n == UNITS:
                    scale_residual(2 * (PAIRS - 3))
                if n == UNITS + 1:
                    scale_residual(2 * (PAIRS - 3) + 1)
                tanh_z(n - 2)
                if n == UNITS - 1:
                    for b in range(2 * (PAIRS - 3)):
                        scale_residual(b)
            for b in range(2 * (PAIRS - 2), B - 1):
                scale_residual(b)

        @block.vector
        def _(dve):
            nc.vector.memset(ones[:, :], 1.0).then_inc(ones_done, 1)
            nc.vector.memset(k_st[1][64:P, :, :].bitcast(FP32), 0.0).then_inc(k1_zeroed, 1)

            def low_part(dst, psum, hi, hi_done, count, done):
                dve.wait_ge(hi_done, count)
                nc.vector.tensor_tensor(dst, psum, hi.bitcast(FP32), ALU.subtract).then_inc(done, 1)

            def weight_lo(i):
                w = W_ORDER[i]
                low_part(weight_columns(wkv_lo, w), weight_rows(weight_bank[i], w), weight_columns(wkv_hi, w), w_t_copied, i + 1, w_lo_done)

            flat = lambda x: x.rearrange("p c s -> p (c s)")

            def prepare_values():
                weight_lo(2)
                dve.wait_ge(bias_in, 16 * 6)
                for ci in range(C):
                    nc.vector.tensor_scalar(x2n[:, ci, 0:P], ones[:, :], bv_col[:, ci:ci + 1], None, ALU.mult).then_inc(bv_repeated, 1)

            def prepare_gates():
                dve.wait_ge(wo_bv_ready, 1)
                dve.wait_ge(gates_in, 16 * 6)
                nc.vector.tensor_tensor(bo_bc[:, :], bo_bc[:, :], misc[0][:, 0:D], ALU.add).then_inc(wo_bv_added, 1)
                dve.wait_ge(tanh_done, 1)
                dve.wait_ge(wo_bv_added, 1)
                nc.vector.tensor_scalar(bo_bc[:, :], bo_bc[:, :], tanh_g[:, 0:1], None, ALU.mult).then_inc(gates_ready, 1)

            def prepare_ffn():
                dve.wait_ge(small_in, 16 * 10)
                nc.vector.tensor_scalar(gw3_rep[:, :], ones[0:64, :], gw3_col[:, :], None, ALU.mult)
                nc.vector.tensor_scalar(half_b[:, :], scal[:, 3:5], 0.5, None, ALU.mult)
                nc.vector.tensor_scalar(gain[:, 0:1], scal[:, 2:3], 0.3, None, ALU.mult)
                nc.vector.tensor_scalar(gain[:, 1:2], scal[:, 2:3], 0.7, None, ALU.mult)
                nc.vector.memset(sign[0:64, 0:1], 1.0)
                nc.vector.memset(sign[64:P, 0:1], -1.0)
                nc.vector.memset(sign[0:64, 1:2], -1.0)
                nc.vector.memset(sign[64:P, 1:2], 1.0).then_inc(prep_done, 1)

            def split_w1(j):
                if j == 0:
                    dve.wait_ge(params_in, 16 * 5)
                    dve.wait_ge(prep_done, 1)
                moved, ci = divmod(j % 4, C)
                cols = slice(moved * D, (moved + 1) * D)
                factor = (sign[:, 1 - ci:2 - ci] if moved else ones[:, 0:1])
                w1_rows = w1_sb[:, 1 - ci if moved else ci, :]
                if j < 4:
                    nc.vector.tensor_scalar(uv_hi[:, ci, cols], w1_rows, factor, None, ALU.mult).then_inc(w1_hi_done, 1)
                else:
                    dve.wait_ge(w1_hi_done, 4)
                    nc.vector.scalar_tensor_tensor(uv_lo[:, ci, cols], w1_rows, factor,
                                                   uv_hi[:, ci, cols].bitcast(FP32), ALU.mult, ALU.subtract)

            def max_of(b, j):
                for t in range(TC):
                    dve.wait_ge(s1_ready, b.count(16, 2 * j + t + 1))
                    nc.vector.tensor_reduce(neg_max[:, j // 4, 2 * (j % 4):2 * (j % 4) + 2, t],
                                            s1_bank[t][:, :].rearrange("p (e s) -> p e s", e=2),
                                            AX.X, ALU.max, negate=True).then_inc(s1_maxed, 1)

            def split_max(at, c, stats_of=None):
                if stats_of:
                    dve.wait_ge(x_loaded[stats_of.u], stats_of.count_of_parity(16))
                    for t in range(TC):
                        nc.vector.bn_stats(stats[:, t, :], x_in[:, bass.ds(stats_of.n(), 1), t, :].rearrange("p b d -> p (b d)"))
                if at:
                    if at.turn is not None or at.base >= 1:
                        dve.wait_ge(max_tp_ready, at.count(2, c - 1))
                    nm = neg_max[:, c, :, :].rearrange("p h t -> p (h t)")
                    hi, lo = (max_parts[:, c, i, :, :].rearrange("p h t -> p (h t)") for i in range(2))
                    dve.wait_ge(s1_maxed, at.count(16, 8 * (c + 1)))
                    nc.vector.tensor_copy(hi, nm)
                dve.drain()
                if at:
                    nc.vector.tensor_tensor(lo, nm, hi.bitcast(FP32), ALU.subtract).then_inc(max_parts_done, 1)
                if stats_of:
                    for t in range(TC):
                        nc.vector.bn_aggr(mean_var[:, t, :], stats[:, t, :]).then_inc(aggr_done, 1)

            def project_lo(at, i, hi, lo, hi_done, done, psum):
                dve.wait_ge(hi_done, at.count(2, 2))
                for c in range(C):
                    nc.vector.scalar_tensor_tensor(lo[:, at.u, c, :], psum[:, c * S:(c + 1) * S], bqk[:, i, c:c + 1],
                                                   hi[:, at.u, c, :].bitcast(FP32), ALU.add, ALU.subtract).then_inc(done, 1)

            def norm_outputs(d, half):
                dve.wait_ge(o_tp_ready, d.count(2, half + 1))
                src = misc[0][:, :].rearrange("p (t h e) -> p t h e", t=TC, e=SLOT)
                rd = rden[:, :, :, :].rearrange("p t g i -> p t (g i)")
                nc.vector.reciprocal(rd, src[:, :, :, DK]).then_inc(rden_done, 1)
                dve.wait_ge(rden_done, d.count(2, half + 1))
                if half == 0 and (d.turn is not None or d.base >= 1):
                    dve.wait_ge(o_nt_ready, d.count(1, 0))
                nc.vector.tensor_tensor(o_n[:, :, half * P:(half + 1) * P].rearrange("p t (h e) -> p t h e", e=DK),
                                        src[:, :, :, 0:DK], rd.unsqueeze(3).to_broadcast([P, TC, HC, DK]),
                                        ALU.mult).then_inc(o_normed, 1)

            def split_lo(p):
                for ci in range(C):
                    dve.wait_ge(x_hi_done, 2 * p + ci + 1)
                    nc.vector.tensor_tensor(x_lo[p % 2][ci], state[:, 2 * p:2 * p + 2, ci, :],
                                            x_hi[p % 2][ci].bitcast(FP32), ALU.subtract).then_inc(x_parts_done, 1)

            def statistics(src, out_stats, out_mean_var, done):
                for t in range(TC):
                    nc.vector.bn_stats(out_stats[:, t, :], src(t))
                dve.drain()
                for t in range(TC):
                    nc.vector.bn_aggr(out_mean_var[:, t, :], out_stats[:, t, :]).then_inc(done, 1)

            def normalize(st, a, x_of):
                low_part(flat(ct_lo[:, a.u, :, :]), misc[1][:, :], flat(ct_hi[:, a.u, :, :]), ct_hi_done, a.count(1, 1), ct_lo_done)
                dve.wait_ge(rstd_done, a.count(1, 1))
                if a.turn is not None or a.base >= 1:
                    dve.wait_ge(x_tp_ready, a.count(1, 0))
                for t in range(TC):
                    last = nc.vector.tensor_scalar(xn[:, t, :], x_of(t), mean_var[:, t, 0:1], rstd[:, t:t + 1],
                                                   ALU.subtract, ALU.mult)
                last.then_inc(xn_done, 1)

            def step(st):
                a, b, c, d = (st.batch(x) for x in STAGES)
                early = st.turn is None and st.base == 1
                x_of = lambda t: x_in[:, bass.ds(a.n(), 1), t, :].rearrange("p b d -> p (b d)")
                x2_of = lambda t: x2[:, bass.ds(d.n(), 1), t, :].rearrange("p b d -> p (b d)")
                for j in range(8):
                    if j == 0:
                        if a or c:
                            split_max(c, 1, a)
                    if j == 0 and st.turn is None and st.base == 0:
                        weight_lo(0)
                    if j == (0 if early else 1) and a:
                        normalize(st, a, x_of)
                    if j == 0 and early:
                        prepare_values()
                    if j == (0 if early else 2) and a:
                        project_lo(a, 1, k_hi, k_lo, k_hi_done, k_lo_done, misc[1])
                    if j == (2 if early else 4):
                        if a:
                            project_lo(a, 0, q_hi, q_lo, q_hi_done, q_lo_done, query_bank(a))
                    if j == 4 and b:
                        split_max(b, 0)
                    if j == 5 and d:
                        dve.wait_ge(y_ready, d.count(1, 1))
                        dve.wait_ge(xb_done, d.count(2, 2))
                        nc.vector.scalar_tensor_tensor(x2[:, bass.ds(d.n(), 1), :, :].rearrange("p b t d -> p (b t d)"),
                                                       misc[0][:, :], tanh_g[:, 0:1], x_b[:, :, :].rearrange("p t d -> p (t d)"),
                                                       ALU.mult, ALU.add).then_inc(x2_done, 1)
                        dve.drain()
                        statistics(x2_of, stats2, mean_var2, aggr2_done)
                    if j == 6 and d:
                        dve.wait_ge(rstd2_done, d.count(1, 1))
                        for t in range(TC):
                            last = nc.vector.tensor_scalar(x2n[:, t, :], x2_of(t), mean_var2[:, t, 0:1], rstd2[:, t:t + 1],
                                                           ALU.subtract, ALU.mult)
                        last.then_inc(x2n_done, 1)
                        b_of = bass.ds(d.n(), 1)
                        nc.vector.tensor_copy(mean_all[:, b_of, :].rearrange("p b t -> p (b t)"), mean_var2[:, :, 0])
                        nc.vector.tensor_copy(rstd_all[:, b_of, :].rearrange("p b t -> p (b t)"), rstd2[:, :]).then_inc(stats_kept, 1)
                    if b:
                        max_of(b, j)
                    if j == 1 and d:
                        norm_outputs(d, 0)
                    if j == 2 and d:
                        norm_outputs(d, 1)
                    if st.turn is None and st.base == B:
                        split_w1(j)
                    work = uv_work(st, j)
                    if work and work[1] is None:
                        split_lo(work[0])
                if st.turn is None:
                    if st.base == 2:
                        prepare_gates()
                    if st.base == 3:
                        prepare_ffn()

            run_steps(dve, step)

            dve.wait_ge(gl_done, 3)
            nc.vector.tensor_scalar(base_c[:, :], gz[:, :], gain[:, 1:2], 0.1, ALU.mult, ALU.add).then_inc(base_done, 1)
            dve.wait_ge(base_done, 1)

            def tt(dst, x, y, op):
                return nc.vector.tensor_tensor(dst, x, y, op)

            def finish_pair(p):
                for half in range(2) if p < PAIRS - 1 else (1, 0):
                    b = 2 * p + half
                    if b == B - 1:
                        dve.wait_ge(tw_done, B)
                        dve.wait_ge(coefficients_done, PAIRS)
                        for t in range(TC):
                            nc.vector.tensor_scalar(x2[:, b, t, :], x2[:, b, t, :], out_scale[:, p, half, t:t + 1],
                                                    out_shift[:, p, half, t:t + 1], ALU.mult, ALU.add)
                        dve.drain()
                    for t in range(TC):
                        if b < B - 1:
                            dve.wait_ge(out_scaled, TC * b + t + 1)
                        nc.vector.scalar_tensor_tensor(x2[:, b, t, :], tw[:, b, t, :], g_beta3[:, p, half, t:t + 1],
                                                       x2[:, b, t, :], ALU.mult, ALU.add).then_inc(fin_done, 1)

            u_of = lambda p, k: uv[p][k][:, 0:D]
            v_of = lambda p, k: uv[p][k][:, D:2 * D]
            column = lambda x, k: x[:, k // TC, k % TC:k % TC + 1]

            def turn_v(p):
                for k in range(TP):
                    nc.vector.scalar_tensor_tensor(v_of(p, k), u_of(p, k), column(minus_c1[:, p, :, :], k), v_of(p, k),
                                                   ALU.mult, ALU.add)

            for n in range(UNITS):
                cycle, p = divmod(n, PAIRS)
                c, c1, r = coup[:, n, :, :], coup[:, p, :, :], rstd_all[:, 2 * p:2 * p + 2, :]
                dve.wait_ge(tanh_z_done, n + 1)
                nc.vector.scalar_tensor_tensor(c, tz[:, n, :, :], gain[:, 0:1],
                                               base_c[:, 2 * p:2 * p + 2].unsqueeze(2).to_broadcast([P, 2, TC]), ALU.mult, ALU.add)
                dve.drain()
                if cycle < CYCLES - 1:
                    for k in range(TP):
                        last = nc.vector.scalar_tensor_tensor(mixed[:, p, k, :], v_of(p, k), column(c, k),
                                                              u_of(p, k) if cycle == 0 else mixed[:, p, k, :], ALU.mult, ALU.add)
                    last.then_inc(mixed_done, 1)
                if cycle == 0:
                    nc.vector.tensor_scalar(minus_c1[:, p, :, :], c1, -1.0, None, ALU.mult)
                    dve.drain()
                    turn_v(p)
                if cycle == 1:
                    tt(prod[:, p, 0, :, :], c, c1, ALU.mult)
                    tt(beta2[:, p, :, :], c, c1, ALU.add)
                    dve.drain()
                    nc.vector.tensor_scalar(alpha2[:, p, :, :], prod[:, p, 0, :, :], -1.0, 1.0, ALU.mult, ALU.add)
                    dve.drain()
                    nc.vector.tensor_scalar(g_alpha2[:, p, :, :], alpha2[:, p, :, :], tanh_g[:, 1:2], None, ALU.mult)
                    nc.vector.tensor_scalar(g_beta2[:, p, :, :], beta2[:, p, :, :], tanh_g[:, 1:2], None, ALU.mult)
                    dve.drain()
                    tt(gr_alpha2[:, p, :, :], g_alpha2[:, p, :, :], r, ALU.mult)
                    tt(gr_beta2[:, p, :, :], g_beta2[:, p, :, :], r, ALU.mult)
                if cycle == 2:
                    tt(prod[:, p, 1, :, :], c, gr_beta2[:, p, :, :], ALU.mult)
                    tt(prod[:, p, 2, :, :], c, g_alpha2[:, p, :, :], ALU.mult)
                    dve.drain()
                    tt(gr_alpha3[:, p, :, :], gr_alpha2[:, p, :, :], prod[:, p, 1, :, :], ALU.subtract)
                    tt(g_beta3[:, p, :, :], g_beta2[:, p, :, :], prod[:, p, 2, :, :], ALU.add)
                    dve.drain()
                    nc.vector.tensor_scalar(out_scale[:, p, :, :], gr_alpha3[:, p, :, :], 1.0, None, ALU.add)
                    nc.vector.scalar_tensor_tensor(out_shift[:, p, :, :], gr_alpha3[:, p, :, :], -1.0, mean_all[:, 2 * p:2 * p + 2, :],
                                                   ALU.mult, ALU.mult).then_inc(coefficients_done, 1)
                    if p >= 1:
                        finish_pair(p - 1)
            finish_pair(PAIRS - 1)


_INS = ['x', 'ctx_1024', 'g_xattn', 'g_ffn', 'L0_xattn_Wq', 'L0_xattn_bq', 'L0_xattn_Wk', 'L0_xattn_bk',
        'L0_xattn_Wv', 'L0_xattn_bv', 'L0_xattn_Wo', 'L0_xattn_bo',
        'L0_ffn_cn_w1', 'L0_ffn_cn_b1', 'L0_ffn_cn_w2', 'L0_ffn_cn_b2', 'L0_ffn_cn_w3', 'L0_ffn_cn_b3',
        'L0_ffn_cn_w4', 'L0_ffn_cn_b4', 'L0_ffn_gc_w1', 'L0_ffn_gc_b1', 'L0_ffn_gc_w2', 'L0_ffn_gc_b2',
        'L0_ffn_gc_w3', 'L0_ffn_gc_b3', 'L0_ffn_adaptive_range']


def kernel(**inputs):
    import numpy as _np
    import concourse.bacc as _bacc
    from concourse import mybir as _mybir
    from concourse.bass_utils import run_bass_kernel_spmd as _run

    nc = _bacc.Bacc("TRN2", target_bir_lowering=False, num_devices=1)
    arrays, args = {}, []
    for name in _INS:
        a = _np.ascontiguousarray(inputs[name])
        arrays[f"in_{name}_dram"] = a
        args.append(nc.dram_tensor(f"in_{name}_dram", a.shape, _mybir.dt.from_np(a.dtype), kind="ExternalInput").ap())
    args.append(nc.dram_tensor("out_0_dram", (B, S, D), _mybir.dt.float32, kind="ExternalOutput").ap())
    build(nc, *args)
    r = _run(nc, [arrays], core_ids=[0])
    return r.results[0]["out_0_dram"]
```
